# Optimizing a Trainium2 kernel written in Bass

```python
import numpy as np
import jax
import jax.numpy as jnp

def _softmax(x, axis=-1):
    return jax.nn.softmax(x, axis=axis)

def _gelu(x):
    return jax.nn.gelu(x, approximate=True)

def _silu(x):
    return jax.nn.silu(x)

def _sigmoid(x):
    return jax.nn.sigmoid(x)

def _layernorm(x, axis=-1, eps=1e-05):
    m = jnp.mean(x, axis=axis, keepdims=True)
    v = jnp.var(x, axis=axis, keepdims=True)
    return (x - m) / jnp.sqrt(v + eps)

def _scatter_add(tgt, idx, src, axis=0):
    return tgt.at[idx].add(src)

def _segment_sum(src, seg, n):
    return jax.ops.segment_sum(src, seg, n)
kernel_name = 'mk_seq_preln_d1_jaxref_r8_1a4176'

def setup_inputs(seed: int=0):
    np.random.seed(seed)
    _w = jnp.asarray

    def _L0_attn_setup():
        import jax, jax.numpy as jnp
        import numpy as np
        NUM_HEADS = 8
        MAXLEN = 256
        NEG = -4294967295.0

        def silu(x):
            return x * jax.nn.sigmoid(x)
        key = jax.random.key(seed)
        ks = jax.random.split(key, 6)
        B, S, D = (4, 256, 128)
        std = 0.02
        return {'x': jax.random.normal(ks[0], (B, S, D), jnp.float32), 'Wq': jax.random.normal(ks[1], (D, D), jnp.float32) * std, 'Wk': jax.random.normal(ks[2], (D, D), jnp.float32) * std, 'Wv': jax.random.normal(ks[3], (D, D), jnp.float32) * std, 'Wu': jax.random.normal(ks[4], (D, D), jnp.float32) * std, 'rel_bias': jax.random.normal(ks[5], (2 * MAXLEN - 1, NUM_HEADS), jnp.float32) * std}
    _L0_attn_in = _L0_attn_setup()

    def _L0_ffn_setup():
        import jax, jax.numpy as jnp
        import numpy as np
        D_MODEL = 128
        HIDDEN = 512
        NUM_EXPERTS = 8
        TOP_K = 2
        key = jax.random.key(seed)
        k_x, k_g, k_in, k_out = jax.random.split(key, 4)
        bound_in = 1.0 / HIDDEN
        bound_out = 1.0 / D_MODEL
        x = jax.random.normal(k_x, (2, 256, D_MODEL), dtype=jnp.float32)
        w_gate = jax.random.uniform(k_g, (NUM_EXPERTS, D_MODEL), dtype=jnp.float32, minval=-D_MODEL ** (-0.5), maxval=D_MODEL ** (-0.5))
        w_in = jax.random.uniform(k_in, (NUM_EXPERTS, HIDDEN, D_MODEL), dtype=jnp.float32, minval=-bound_in, maxval=bound_in)
        w_out = jax.random.uniform(k_out, (NUM_EXPERTS, D_MODEL, HIDDEN), dtype=jnp.float32, minval=-bound_out, maxval=bound_out)
        return {'x': x, 'w_gate': w_gate, 'w_in': w_in, 'w_out': w_out}
    _L0_ffn_in = _L0_ffn_setup()
    _d = {'L0_attn_x': _L0_attn_in['x'], 'L0_attn_Wq': _L0_attn_in['Wq'], 'L0_attn_Wk': _L0_attn_in['Wk'], 'L0_attn_Wv': _L0_attn_in['Wv'], 'L0_attn_Wu': _L0_attn_in['Wu'], 'L0_attn_rel_bias': _L0_attn_in['rel_bias'], 'L0_ffn_w_gate': _L0_ffn_in['w_gate'], 'L0_ffn_w_in': _L0_ffn_in['w_in'], 'L0_ffn_w_out': _L0_ffn_in['w_out']}
    _x0 = _d['L0_attn_x']
    _d['L0_attn_x'] = jax.random.normal(jax.random.fold_in(jax.random.key(seed), 1), (4, 1024, 128), dtype=_x0.dtype)
    del _x0
    return _d

def reference(L0_attn_x, L0_attn_Wq, L0_attn_Wk, L0_attn_Wv, L0_attn_Wu, L0_attn_rel_bias, L0_ffn_w_gate, L0_ffn_w_in, L0_ffn_w_out):

    def _L0_attn_ref(x, Wq, Wk, Wv, Wu, rel_bias):
        import jax, jax.numpy as jnp
        import numpy as np
        NUM_HEADS = 8
        MAXLEN = 256
        NEG = -4294967295.0

        def silu(x):
            return x * jax.nn.sigmoid(x)
        B, S, D = x.shape
        H = NUM_HEADS
        hd = D // H
        Q = (x @ Wq).reshape(B, S, H, hd).transpose(0, 2, 1, 3)
        K = (x @ Wk).reshape(B, S, H, hd).transpose(0, 2, 1, 3)
        V = (x @ Wv).reshape(B, S, H, hd).transpose(0, 2, 1, 3)
        U = x @ Wu
        Q, K, V = (silu(Q), silu(K), silu(V))
        scores = jnp.einsum('bhsd,bhtd->bhst', Q, K)
        pos = jnp.arange(S)
        rel_idx = pos[:, None] - pos[None, :] + MAXLEN - 1
        bias = rel_bias[rel_idx]
        scores = scores + bias.transpose(2, 0, 1)[None]
        scores = scores / jnp.sqrt(jnp.asarray(hd, jnp.float32))
        causal = jnp.tril(jnp.ones((S, S), jnp.float32))
        scores = jnp.where(causal[None, None] == 0, NEG, scores)
        key_mask = jnp.sign(jnp.abs(K).sum(-1))
        scores = jnp.where(key_mask[:, :, None, :] == 0, NEG, scores)
        weights = silu(scores)
        attn = jnp.einsum('bhst,bhtd->bhsd', weights, V)
        attn = attn.transpose(0, 2, 1, 3).reshape(B, S, D)
        return attn * silu(U)

    def _L0_ffn_ref(x, w_gate, w_in, w_out):
        import jax, jax.numpy as jnp
        import numpy as np
        D_MODEL = 128
        HIDDEN = 512
        NUM_EXPERTS = 8
        TOP_K = 2
        B, S, D = x.shape
        E = w_in.shape[0]
        xt = x.reshape(-1, D)
        logits = (xt @ w_gate.T).astype(jnp.float32)
        top_logits, top_idx = jax.lax.top_k(logits, TOP_K)
        top_gates = jax.nn.softmax(top_logits, axis=-1).astype(x.dtype)
        gates = (jax.nn.one_hot(top_idx, E, dtype=x.dtype) * top_gates[..., None]).sum(axis=1)
        y = jnp.zeros_like(xt)
        for e in range(E):
            h = xt @ w_in[e].T
            y = y + gates[:, e:e + 1] * (h @ w_out[e].T)
        return y.reshape(B, S, D)
    x = L0_attn_x
    x = x + _L0_attn_ref(_layernorm(x, axis=-1), L0_attn_Wq, L0_attn_Wk, L0_attn_Wv, L0_attn_Wu, L0_attn_rel_bias)
    x = x + _L0_ffn_ref(_layernorm(x, axis=-1), L0_ffn_w_gate, L0_ffn_w_in, L0_ffn_w_out)
    return x

_drawn_inputs = setup_inputs


def setup_inputs(seed=0):
    import zlib

    import numpy as np

    out = dict(_drawn_inputs(seed))
    spreads = {}
    factors = {'L0_attn_Wq': 8.0,
     'L0_attn_Wk': 8.0,
     'L0_attn_Wv': 8.0,
     'L0_attn_Wu': 8.0,
     'L0_attn_rel_bias': 8.0,
     'L0_ffn_w_gate': 200.0,
     'L0_ffn_w_in': 200.0,
     'L0_ffn_w_out': 200.0}
    for name, (base, spread) in spreads.items():
        noise = np.random.default_rng([zlib.crc32(name.encode()), seed]).standard_normal(out[name].shape)
        drawn = base * np.exp(spread * noise) if base else spread * noise
        out[name] = jnp.asarray(drawn.astype(out[name].dtype))
    for name, factor in factors.items():
        out[name] = (out[name] * factor).astype(out[name].dtype)
    return out
```

```python
from contextlib import ExitStack

import concourse.bass as bass
from concourse import mybir

P = 128
B, S, D = 4, 1024, 128
H, HD = 8, 16
E, HID = 8, 512
MAXLEN = 256
NEG = -4294967295.0
EPS = 1e-5
NT = S // P
QUADS = H // 4
BANK = 512
NEAR = P + MAXLEN
HC = HID // P

F32 = mybir.dt.float32
F32R = mybir.dt.float32r
BF16 = mybir.dt.bfloat16
ALU = mybir.AluOpType
ACT = mybir.ActivationFunctionType
AX = mybir.AxisListType.X

GROUPS = []
for _kb in range(NT):
    for _bank in range(S // BANK):
        _q0 = max(_kb * P, _bank * BANK)
        if _q0 < (_bank + 1) * BANK:
            GROUPS.append((_kb, _q0, (_bank + 1) * BANK - _q0))
NG = len(GROUPS)
LAST_IN_BANK0 = max(i for i, (_, q0, _) in enumerate(GROUPS) if q0 < BANK)


def plan_timeline():
    slots = [(None, [("stats1", 0)]), (None, [("norm1", 0)]), (None, [("T1", 0, 0), ("T1", 0, 1)]),
             (None, [("Q", 0, 0), ("Q", 0, 1), ("K", 0, 0), ("K", 0, 1), ("split", 0, 0), ("split", 0, 1)]),
             (None, [("VU", 0, i) for i in range(4)] + [("MASK", 0)] + [("FLIP", i) for i in range(H * NEAR // BANK)])]
    per = QUADS * NG
    for b in range(B):
        jobs = [[] for _ in range(per)]
        if b + 1 < B:
            n = b + 1
            jobs[0] += [("stats1", n)]
            jobs[2] += [("norm1", n)]
            jobs[3] += [("T1", n, 0), ("T1", n, 1)]
            jobs[4] += [("Q", n, 0), ("Q", n, 1)]
            jobs[5] += [("K", n, 0), ("K", n, 1)]
            jobs[6] += [("split", n, 0)]
            jobs[7] += [("split", n, 1)]
            jobs[6] += [("VU", n, 0)]
            jobs[7] += [("VU", n, 1)]
            jobs[8] += [("VU", n, 2)]
            jobs[9] += [("VU", n, 3)]
            jobs[10] += [("MASK", n)]
        if b > 0:
            n = b - 1
            jobs[0] += [("SEL", n, 0), ("SEL", n, 1)]
            jobs[2] += [("stats2", n)]
            jobs[4] += [("norm2", n)]
            jobs[5] += [("T2", n, 0), ("T2", n, 1)]
            jobs[6] += [("LOG", n)]
            for t in range(NT):
                for half in range(2):
                    jobs[per - 2 * NT + 2 * t + half] += [("FF", n, t, half)]
        else:
            for e in range(E):
                jobs[8 + 2 * e] += [("WT", e)]
                jobs[9 + 2 * e] += [("M", e)]
        slots += [((b, g // NG, g % NG), jobs[g]) for g in range(per)]
    n = B - 1
    slots += [(None, [("SEL", n, 0), ("SEL", n, 1)]), (None, [("stats2", n)]), (None, [("norm2", n)]),
              (None, [("T2", n, 0), ("T2", n, 1)]), (None, [("LOG", n)]),
              (None, [("FF", n, t, half) for t in range(NT) for half in range(2)])]
    return slots


TIMELINE = plan_timeline()
BANKED = ("T1", "Q", "K", "VU", "MASK", "SEL", "T2", "LOG", "FF", "WT", "M", "FLIP")
NUMBER = {}
for _group, _jobs in TIMELINE:
    for _j in _jobs:
        if _j[0] in BANKED:
            NUMBER[_j] = len(NUMBER)


def order(b, quad, g):
    return (b * QUADS + quad) * NG + g


def build(nc, x, Wq, Wk, Wv, Wu, rel_bias, w_gate, w_in, w_out, out):
    with ExitStack() as ctx:
        def sb(name, shape, dt=F32):
            return ctx.enter_context(nc.sbuf_tensor(name, shape, dt))

        def sem(name):
            return ctx.enter_context(nc.semaphore(name))

        xs = sb("xs", [P, B, NT, D])
        xn1 = sb("xn1", [P, NT, D])
        xn1T = sb("xn1T", [P, S])
        xn2 = sb("xn2", [P, NT, D])
        xn2T = sb("xn2T", [P, S])
        qk32 = [sb("q32", [P, S]), sb("k32", [P, S])]
        hi = [sb("q_hi", [P, S], F32R), sb("k_hi", [P, S], F32R)]
        lo = [sb("q_lo", [P, S], F32R), sb("k_lo", [P, S], F32R)]
        kabs = sb("kabs", [P, S], BF16)
        q_stack = sb("q_stack", [P, H // 2, S], F32R)
        k_stack = sb("k_stack", [P, H, S], F32R)
        vu = sb("vu", [P, 2, NT, 2 * D])
        v_pad = sb("v_pad", [P, 2, NT, H, 32])
        kmask = sb("kmask", [P, NT, H])
        wts = sb("wts", [P, 2, 4, BANK])
        bias_rev = wts[:].rearrange("p a j c -> p (a j c)")[:, 0:H * NEAR]
        oT = sb("oT", [P, QUADS, S])
        gated = xn2
        bias_near = sb("bias_near", [P, H, NEAR])
        far_row = sb("far_row", [P, H])
        far = sb("far", [P, H])
        ext = sb("ext", [H, BANK + MAXLEN])
        mm_e = sb("mm_e", [P, E, D])
        win_s = sb("win_s", [P, 2, HC, D])
        wout_s = sb("wout_s", [P, 2, HID])
        woutT = sb("woutT", [P, 2, HC, D])
        wq_s, wk_s, wvu_s = sb("wq_s", [P, D]), sb("wk_s", [P, D]), sb("wvu_s", [P, 2 * D])
        wg_s = sb("wg_s", [P, E])
        ident = sb("ident", [P, P])
        flip = sb("flip", [P, P])
        sel = sb("sel", [P, QUADS, H, HD])
        headsum = sb("headsum", [P, H], BF16)
        stats = sb("stats", [P, 2, NT, 6])
        mv = sb("mv", [P, 2, NT, 2])
        rstd = sb("rstd", [P, 2, NT])
        eps_t = sb("eps_t", [P, NT])
        mhalf = sb("mhalf", [P, NT])
        rank = sb("rank", [P, 1, E])
        lg = sb("lg", [P, 3, NT, E])
        pick = sb("pick", [P, 2, NT, E])
        top = sb("top", [P, 5, NT])
        gate2 = sb("gate2", [P, 2, NT])
        gates = sb("gates", [P, NT, E])
        ymix = sb("ymix", [P, 2, E, D])
        bias_dram = nc.dram_tensor("bias_dram", [H, BANK], F32, kind="Internal").ap()

        score = [ctx.enter_context(nc.psum_tensor(f"score{j}", [P, BANK], F32)) for j in range(4)]
        o_acc = [ctx.enter_context(nc.psum_tensor(f"o_acc{j}", [P, BANK], F32)) for j in range(2)]
        jobp = [ctx.enter_context(nc.psum_tensor(f"jobp{j}", [P, BANK], F32)) for j in range(2)]

        x_in = [sem(f"x_in{b}") for b in range(B)]
        w_qk_in, w_vu_in, w_g_in = sem("w_qk_in"), sem("w_vu_in"), sem("w_g_in")
        rb_in, far_in, ext_out, bias_in = sem("rb_in"), sem("far_in"), sem("ext_out"), sem("bias_in")
        win_in = [sem(f"win_in{i}") for i in range(2)]
        wout_in = [sem(f"wout_in{i}") for i in range(2)]
        stack_in = [sem(f"stack_in{q}") for q in range(QUADS)]
        stored = sem("stored")
        consts = sem("consts")
        zeroed = sem("zeroed")
        ext_set, ext_ready, far_ready = sem("ext_set"), sem("ext_ready"), sem("far_ready")
        averaged = sem("averaged")
        scaled = sem("scaled")
        normed1, normed2 = sem("normed1"), sem("normed2")
        filled = sem("filled")
        drained = [sem(f"drained{i}") for i in range(2)]
        kabs_ready = sem("kabs_ready")
        hi_ready, lo_ready = sem("hi_ready"), sem("lo_ready")
        v_ready = sem("v_ready")
        scored = [sem(f"scored{j}") for j in range(4)]
        biased = [sem(f"biased{j}") for j in range(4)]
        weighed = [sem(f"weighed{j}") for j in range(4)]
        pv_done = sem("pv_done")
        o_copied = [sem(f"o_copied{i}") for i in range(2)]
        x1_ready = sem("x1_ready")
        top_ready, tanh_ready, gates_ready = sem("top_ready"), sem("tanh_ready"), sem("gates_ready")
        tile_done = sem("tile_done")
        dve_step, pool_step = sem("dve_step"), sem("pool_step")

        def wait_filled(eng, job):
            eng.wait_ge(filled, NUMBER[job] + 1)

        def wait_drained(eng, job):
            n = NUMBER[job]
            eng.wait_ge(drained[n % 2], n // 2 + 1)

        def bank_of(job):
            return jobp[NUMBER[job] % 2]

        def drained_by(ins, job):
            ins.then_inc(drained[NUMBER[job] % 2], 1)

        block = ctx.enter_context(nc.Block())

        @block.sync
        def _(sp):
            def load_x(b):
                sp.dma_start(xs[:, b], x[b].rearrange("(t p) d -> p t d", p=P)).then_inc(x_in[b], 16)

            def load_expert(e):
                if e >= 2:
                    wait_filled(sp, ("M", e - 2))
                sp.dma_start(win_s[:, e % 2], w_in[e].rearrange("(c p) d -> p c d", p=P)).then_inc(win_in[e % 2], 16)
                sp.dma_start(wout_s[:, e % 2], w_out[e]).then_inc(wout_in[e % 2], 16)

            def load_stack(b, quad):
                for side, stack in ((0, q_stack), (1, k_stack)):
                    if b > 0 and side == 0:
                        for j in range(4):
                            sp.wait_ge(scored[j], order(b - 1, quad, NG - 1) + 1)
                    if b == 0 and side == 1:
                        sp.wait_ge(zeroed, 3)
                    sp.wait_ge(hi_ready, 4 * b + 2 * side + 2)
                    sp.wait_ge(lo_ready, 4 * b + 2 * side + 2)
                    for k in range(4):
                        part = (hi, lo)[(k % 2, k // 2)[side]][side]
                        for h in range(4 * quad, 4 * quad + 4):
                            row = 64 * (h % 2) + HD * k
                            sp.dma_start(stack[row:row + HD, h if side else h // 2, :].bitcast(F32),
                                         part[HD * h:HD * h + HD, :].bitcast(F32)).then_inc(stack_in[quad], 16)

            def store(b, half):
                sp.wait_ge(tile_done, NT * b + (NT // 2) * (half + 1))
                t0 = half * NT // 2
                sp.dma_start(out[b].rearrange("(t p) d -> p t d", p=P)[:, t0:t0 + NT // 2],
                             xs[:, b, t0:t0 + NT // 2]).then_inc(stored, 16)

            load_x(0)
            sp.dma_start(wq_s[:], Wq).then_inc(w_qk_in, 16)
            sp.dma_start(wk_s[:], Wk).then_inc(w_qk_in, 16)
            sp.dma_start(ext[:, BANK:BANK + MAXLEN], rel_bias[MAXLEN - 1:, :].rearrange("r h -> h r"),
                         allow_slow_non_contiguous=True).then_inc(rb_in, 16)
            sp.dma_start(far_row[:], rel_bias[2 * MAXLEN - 2:, :].to_broadcast([P, H])).then_inc(far_in, 16)
            sp.dma_start(wvu_s[:, 0:D], Wv).then_inc(w_vu_in, 16)
            sp.dma_start(wvu_s[:, D:], Wu).then_inc(w_vu_in, 16)
            sp.dma_start(wg_s[:], w_gate.rearrange("e d -> d e"), allow_slow_non_contiguous=True).then_inc(w_g_in, 16)
            sp.wait_ge(ext_ready, 1)
            sp.dma_start(bias_dram, ext[:, 0:BANK]).then_inc(ext_out, 16)
            sp.wait_ge(ext_out, 16)
            sp.dma_start(bias_rev.rearrange("p (h c) -> p h c", h=H),
                         bass.AP(bias_dram.tensor, 0, [[1, P], [BANK, H], [1, NEAR]])).then_inc(bias_in, 16)
            load_stack(0, 0)
            load_stack(0, 1)
            load_x(1)
            load_expert(0)
            load_expert(1)
            load_x(2)
            load_x(3)
            for e in range(2, E):
                load_expert(e)
            for b in range(1, B + 1):
                if b < B:
                    load_stack(b, 0)
                if b > 1:
                    store(b - 2, 0)
                if b < B:
                    load_stack(b, 1)
                if b > 1:
                    store(b - 2, 1)
            store(B - 1, 0)
            store(B - 1, 1)
            sp.wait_ge(stored, 16 * 2 * B)

        @block.gpsimd
        def _(pool):
            step = [0]

            def then_wait(ins):
                step[0] += 1
                ins.then_inc(pool_step, 1)
                pool.wait_ge(pool_step, step[0])

            pool.memset(eps_t[:], EPS).then_inc(consts, 1)
            pool.memset(mhalf[:], -0.5).then_inc(consts, 1)
            then_wait(pool.memset(ident[:], 0.0))
            pool.affine_select(out=ident[:], in_=ident[:], compare_op=ALU.not_equal, fill=1.0, base=0,
                               pattern=[[-1, P]], channel_multiplier=1).then_inc(consts, 1)
            pool.wait_ge(consts, 3)
            for half in range(2):
                pool.memset(k_stack[64 * (1 - half):64 * (2 - half), half:H:2, :].bitcast(F32), 0.0).then_inc(zeroed, 1)
                pool.wait_ge(zeroed, half + 1)
            pool.memset(v_pad[:], 0.0).then_inc(zeroed, 1)
            then_wait(pool.memset(headsum[:], 1.0))
            then_wait(pool.affine_select(out=headsum[:], in_=headsum[:], compare_op=ALU.is_ge, fill=0.0, base=0,
                                         pattern=[[-HD, H]], channel_multiplier=1))
            pool.affine_select(out=headsum[:], in_=headsum[:], compare_op=ALU.is_ge, fill=0.0, base=HD - 1,
                               pattern=[[HD, H]], channel_multiplier=-1).then_inc(consts, 1)
            then_wait(pool.memset(flip[:], 0.0))
            pool.affine_select(out=flip[:], in_=flip[:], compare_op=ALU.not_equal, fill=1.0, base=1 - P,
                               pattern=[[1, P]], channel_multiplier=1).then_inc(consts, 1)
            then_wait(pool.memset(sel[:], 0.0))
            for q in range(QUADS):
                pool.affine_select(out=sel[:, q], in_=sel[:, q], compare_op=ALU.not_equal, fill=1.0, base=32 * 4 * q,
                                   pattern=[[-32, H], [-1, HD]], channel_multiplier=1).then_inc(consts, 1)
            for e in range(E):
                pool.memset(rank[:, :, e:e + 1], float(E - e)).then_inc(consts, 1)

            def scale(b, ln):
                n = SCALES.index((b, ln))
                pool.wait_ge(averaged, n + 1)
                if n >= 1:
                    pb = [m for m, (_, l) in enumerate(SCALES[:n]) if l == ln]
                    if pb:
                        pool.wait_ge((normed1, normed2)[ln], len(pb))
                then_wait(pool.tensor_tensor(rstd[:, ln], mv[:, ln, :, 1], eps_t[:], ALU.add))
                pool.tensor_tensor(rstd[:, ln], rstd[:, ln], mhalf[:], ALU.pow).then_inc(scaled, 1)

            def split_lo(b, side):
                for half in range(2):
                    cols = slice(half * BANK, (half + 1) * BANK)
                    pool.wait_ge(hi_ready, 4 * b + 2 * side + half + 1)
                    pool.tensor_tensor(lo[side][:, cols], qk32[side][:, cols], hi[side][:, cols].bitcast(F32),
                                       ALU.subtract).then_inc(lo_ready, 1)

            def mask_v(b):
                wait_drained(pool, ("MASK", b))
                wait_drained(pool, ("VU", b, 3))
                wait_drained(pool, ("VU", b, 2))
                if b == 0:
                    pool.wait_ge(zeroed, 3)
                if b >= 2:
                    pool.wait_ge(pv_done, order(b - 1, 0, 0))
                pool.tensor_tensor(v_pad[:, b % 2, :, :, 0:HD],
                                   vu[:, b % 2, :, 0:D].rearrange("p t (h d) -> p t h d", h=H),
                                   kmask[:].unsqueeze(3).to_broadcast([P, NT, H, HD]), ALU.mult).then_inc(v_ready, 1)

            def add_attention(b, i):
                wait_drained(pool, ("SEL", b, i))
                ts = slice(i * NT // 2, (i + 1) * NT // 2)
                pool.tensor_tensor(xs[:, b, ts], xs[:, b, ts], gated[:, ts], ALU.add).then_inc(x1_ready, 1)

            def add_experts(b, t):
                wait_drained(pool, ("FF", b, t, 0))
                wait_drained(pool, ("FF", b, t, 1))
                y = ymix[:, t % 2]
                n = E // 2
                while n >= 1:
                    then_wait(pool.tensor_tensor(y[:, 0:n], y[:, 0:n], y[:, n:2 * n], ALU.add))
                    n //= 2
                pool.tensor_tensor(xs[:, b, t], xs[:, b, t], y[:, 0], ALU.add).then_inc(tile_done, 1)

            def jobs(i):
                for job in TIMELINE[i][1]:
                    kind = job[0]
                    if kind == "stats1":
                        scale(job[1], 0)
                    elif kind == "stats2":
                        scale(job[1], 1)
                    elif kind == "split":
                        split_lo(job[1], job[2])
                    elif kind == "MASK":
                        mask_v(job[1])
                    elif kind == "SEL":
                        add_attention(job[1], job[2])
                    elif kind == "FF" and job[3] == 1:
                        add_experts(job[1], job[2])

            for i in range(len(TIMELINE)):
                jobs(i)

        @block.tensor
        def _(pe):
            def scores(group):
                b, quad, g = group
                kb, q0, n = GROUPS[g]
                if g == 0:
                    pe.wait_ge(stack_in[quad], 16 * 32 * (b + 1))
                for j in range(4):
                    h = 4 * quad + j
                    if order(*group) > 0:
                        pe.wait_ge(weighed[j], order(*group))
                    pe.matmul(score[j][:, 0:n], k_stack[:, h, kb * P:(kb + 1) * P], q_stack[:, h // 2, q0:q0 + n],
                              start=True, stop=True).then_inc(scored[j], 1)

            def times_v(group):
                b, quad, g = group
                kb, q0, n = GROUPS[g]
                bank, c0 = q0 // BANK, q0 % BANK
                if g == 0 and quad == 0:
                    pe.wait_ge(v_ready, b + 1)
                if kb == 0 and b * QUADS + quad > 0:
                    pe.wait_ge(o_copied[bank], b * QUADS + quad)
                for j in range(4):
                    pe.wait_ge(weighed[j], order(*group) + 1)
                last_kb = LAST_IN_BANK0 if bank == 0 else NG - 1
                for j in range(4):
                    ins = pe.matmul(o_acc[bank][32 * j:32 * j + 32, c0:c0 + n], v_pad[:, b % 2, kb, 4 * quad + j, :],
                                    wts[:, order(*group) % 2, j, 0:n], start=(kb == 0), stop=(g == last_kb))
                ins.then_inc(pv_done, 1)

            def job_pe(job):
                kind, args = job[0], job[1:]
                if kind not in BANKED:
                    return
                n = NUMBER[job]
                bank = jobp[n % 2]
                if n >= 2:
                    pe.wait_ge(drained[n % 2], n // 2)
                if kind in ("T1", "T2"):
                    b, i = args
                    src, ready = (xn1, normed1) if kind == "T1" else (xn2, normed2)
                    if kind == "T1" and b == 0 and i == 0:
                        pe.wait_ge(consts, 3)
                    pe.wait_ge(ready, b + 1)
                    for k in range(4):
                        ins = pe.transpose(bank[:, k * P:(k + 1) * P], src[:, 4 * i + k, :], ident[:])
                elif kind in ("Q", "K"):
                    b, i = args
                    pe.wait_ge(w_qk_in, 32)
                    wait_drained(pe, ("T1", b, i))
                    ins = pe.matmul(bank[:], (wq_s if kind == "Q" else wk_s)[:], xn1T[:, i * BANK:(i + 1) * BANK],
                                    start=True, stop=True)
                elif kind == "VU":
                    b, i = args
                    pe.wait_ge(w_vu_in, 32)
                    for k in range(2):
                        t = 2 * i + k
                        ins = pe.matmul(bank[:, k * 2 * D:(k + 1) * 2 * D], xn1T[:, t * P:(t + 1) * P], wvu_s[:],
                                        start=True, stop=True)
                elif kind == "MASK":
                    if args[0] == 0:
                        pe.wait_ge(consts, 4)
                    pe.wait_ge(kabs_ready, 2 * (args[0] + 1))
                    for t in range(NT):
                        ins = pe.matmul(bank[:, t * H:(t + 1) * H], kabs[:, t * P:(t + 1) * P], headsum[:],
                                        start=True, stop=True)
                elif kind == "SEL":
                    b, i = args
                    if b == 0:
                        pe.wait_ge(consts, 5 + QUADS)
                    for bk in range(2):
                        pe.wait_ge(o_copied[bk], QUADS * (b + 1))
                    for k in range(4):
                        t = 4 * i + k
                        for q in range(QUADS):
                            ins = pe.matmul(bank[:, k * D:(k + 1) * D], oT[:, q, t * P:(t + 1) * P],
                                            sel[:, q].rearrange("p h d -> p (h d)"), start=(q == 0), stop=(q == QUADS - 1))
                elif kind == "LOG":
                    pe.wait_ge(w_g_in, 16)
                    wait_drained(pe, ("T2", args[0], 0))
                    wait_drained(pe, ("T2", args[0], 1))
                    for t in range(NT):
                        ins = pe.matmul(bank[:, t * E:(t + 1) * E], xn2T[:, t * P:(t + 1) * P], wg_s[:],
                                        start=True, stop=True)
                elif kind == "FF":
                    b, t, half = args
                    if b == 0 and t == 0:
                        wait_drained(pe, ("M", E - 1))
                        wait_drained(pe, ("M", E - 2))
                    ins = pe.matmul(bank[:], xn2T[:, t * P:(t + 1) * P],
                                    mm_e[:, half * E // 2:(half + 1) * E // 2, :].rearrange("p e d -> p (e d)"),
                                    start=True, stop=True)
                elif kind == "FLIP":
                    i = args[0]
                    pe.wait_ge(bias_in, 16)
                    pe.wait_ge(consts, 5)
                    ins = pe.matmul(bank[:], flip[:], bias_rev[:, i * BANK:(i + 1) * BANK], start=True, stop=True)
                elif kind == "WT":
                    e = args[0]
                    pe.wait_ge(wout_in[e % 2], 16 * (e // 2 + 1))
                    for c in range(HC):
                        ins = pe.transpose(bank[:, c * P:(c + 1) * P], wout_s[:, e % 2, c * P:(c + 1) * P], ident[:])
                elif kind == "M":
                    e = args[0]
                    pe.wait_ge(win_in[e % 2], 16 * (e // 2 + 1))
                    wait_drained(pe, ("WT", e))
                    for c in range(HC):
                        ins = pe.matmul(bank[:, 0:D], win_s[:, e % 2, c, :], woutT[:, e % 2, c, :],
                                        start=(c == 0), stop=(c == HC - 1))
                ins.then_inc(filled, 1)

            for i, (group, jobs) in enumerate(TIMELINE):
                if i + 1 < len(TIMELINE) and TIMELINE[i + 1][0] and group:
                    scores(TIMELINE[i + 1][0])
                for job in jobs:
                    job_pe(job)
                if i + 1 < len(TIMELINE) and TIMELINE[i + 1][0] and not group:
                    scores(TIMELINE[i + 1][0])
                if group:
                    times_v(group)

        @block.scalar
        def _(act):
            def weigh(group, j):
                b, quad, g = group
                kb, q0, n = GROUPS[g]
                if order(*group) == 0 and j == 0:
                    act.wait_ge(far_ready, 1)
                near = max(0, min(n, kb * P + NEAR - q0))
                if near:
                    act.wait_ge(biased[j], BIASED[order(*group)] + 1)
                else:
                    act.wait_ge(scored[j], order(*group) + 1)
                if order(*group) >= 2 and j == 0:
                    act.wait_ge(pv_done, order(*group) - 1)
                h = 4 * quad + j
                act.activation(wts[:, order(*group) % 2, j, 0:n], score[j][:, 0:n], ACT.Silu,
                               bias=far[:, h:h + 1], scale=HD ** -0.5).then_inc(weighed[j], 1)

            def job_act(job):
                kind, args = job[0], job[1:]
                if kind in ("T1", "T2"):
                    b, i = args
                    dst = xn1T if kind == "T1" else xn2T
                    wait_filled(act, job)
                    if b > 0 and kind == "T2" and i == 0:
                        wait_filled(act, ("FF", b - 1, NT - 1, 1))
                    if b > 0 and kind == "T1" and i == 0:
                        wait_filled(act, ("VU", b - 1, 3))
                    drained_by(act.copy(dst[:, i * BANK:(i + 1) * BANK], bank_of(job)[:]), job)
                elif kind in ("Q", "K"):
                    b, i = args
                    side = int(kind == "K")
                    wait_filled(act, job)
                    if b > 0 and i == 0:
                        act.wait_ge(lo_ready, 4 * b - 2 * (1 - side))
                        if side:
                            wait_filled(act, ("MASK", b - 1))
                    cols = slice(i * BANK, (i + 1) * BANK)
                    drained_by(act.activation(qk32[side][:, cols], bank_of(job)[:], ACT.Silu), job)
                    if side:
                        wait_drained(act, job)
                        act.activation(kabs[:, cols], qk32[1][:, cols], ACT.Abs).then_inc(kabs_ready, 1)
                elif kind == "VU":
                    b, i = args
                    wait_filled(act, job)
                    if b >= 2 and i == 0:
                        act.wait_ge(v_ready, b - 1)
                        wait_drained(act, ("SEL", b - 2, 1))
                        wait_drained(act, ("SEL", b - 2, 0))
                    drained_by(act.activation(vu[:, b % 2, 2 * i:2 * i + 2, :].rearrange("p t d -> p (t d)"),
                                              bank_of(job)[:], ACT.Silu), job)
                elif kind == "LOG":
                    b = args[0]
                    act.wait_ge(top_ready, b + 1)
                    act.activation(gate2[:, 0], top[:, 4], ACT.Tanh, scale=0.5).then_inc(tanh_ready, 1)
                elif kind == "WT":
                    e = args[0]
                    wait_filled(act, job)
                    if e >= 2:
                        wait_filled(act, ("M", e - 2))
                    drained_by(act.copy(woutT[:, e % 2].rearrange("p c d -> p (c d)"), bank_of(job)[:]), job)
                elif kind == "M":
                    wait_filled(act, job)
                    drained_by(act.copy(mm_e[:, args[0], :], bank_of(job)[:, 0:D]), job)

            for i, (group, jobs) in enumerate(TIMELINE):
                if group:
                    weigh(group, 0)
                if i > 0 and TIMELINE[i - 1][0]:
                    for job in TIMELINE[i - 1][1]:
                        job_act(job)
                if group:
                    for j in range(1, 4):
                        weigh(group, j)
                else:
                    for job in jobs:
                        job_act(job)

        @block.vector
        def _(dve):
            step = [0]

            def then_wait(ins):
                step[0] += 1
                ins.then_inc(dve_step, 1)
                dve.wait_ge(dve_step, step[0])

            def add_bias(group):
                b, quad, g = group
                kb, q0, n = GROUPS[g]
                c0 = q0 - kb * P
                near = max(0, min(n, NEAR - c0))
                if near == 0:
                    return
                if order(*group) == 0:
                    for i in range(2):
                        wait_drained(dve, ("FLIP", H * NEAR // BANK - 1 - i))
                for j in range(4):
                    dve.wait_ge(scored[j], order(*group) + 1)
                    dve.tensor_tensor(score[j][:, 0:near], score[j][:, 0:near], bias_near[:, 4 * quad + j, c0:c0 + near],
                                      ALU.add).then_inc(biased[j], 1)

            def copy_outputs(group):
                b, quad, g = group
                if g not in (LAST_IN_BANK0, NG - 1):
                    return
                bank = int(g == NG - 1)
                dve.wait_ge(pv_done, order(*group) + 1)
                if b > 0:
                    wait_filled(dve, ("SEL", b - 1, 1))
                dve.tensor_copy(oT[:, quad, bank * BANK:(bank + 1) * BANK], o_acc[bank][:]).then_inc(o_copied[bank], 1)

            def job_dve(job):
                kind, args = job[0], job[1:]
                if kind in ("stats1", "stats2"):
                    b, ln = args[0], int(kind == "stats2")
                    if ln:
                        dve.wait_ge(x1_ready, 2 * (b + 1))
                    else:
                        dve.wait_ge(x_in[b], 16)
                    for t in range(NT):
                        ins = dve.bn_stats(stats[:, ln, t, :], xs[:, b, t, :])
                    then_wait(ins)
                    for t in range(NT):
                        ins = dve.bn_aggr(mv[:, ln, t, :], stats[:, ln, t, :])
                    ins.then_inc(averaged, 1)
                elif kind in ("norm1", "norm2"):
                    b, ln = args[0], int(kind == "norm2")
                    dve.wait_ge(scaled, SCALES.index((b, ln)) + 1)
                    if b > 0:
                        wait_filled(dve, (("T1", "T2")[ln], b - 1, 1))
                    dst = xn2 if ln else xn1
                    for t in range(NT):
                        ins = dve.tensor_scalar(dst[:, t, :], xs[:, b, t, :], mv[:, ln, t, 0:1], rstd[:, ln, t:t + 1],
                                                ALU.subtract, ALU.mult)
                    ins.then_inc((normed1, normed2)[ln], 1)
                elif kind == "split":
                    b, side = args
                    if b > 0 and side == 0:
                        for q in range(QUADS):
                            dve.wait_ge(stack_in[q], 16 * 32 * b)
                    for half in range(2):
                        cols = slice(half * BANK, (half + 1) * BANK)
                        wait_drained(dve, ("QK"[side], b, half))
                        dve.tensor_copy(hi[side][:, cols], qk32[side][:, cols]).then_inc(hi_ready, 1)
                elif kind == "MASK":
                    b = args[0]
                    wait_filled(dve, job)
                    if b > 0:
                        dve.wait_ge(v_ready, b)
                    drained_by(dve.tensor_scalar(kmask[:].rearrange("p t h -> p (t h)"), bank_of(job)[:, 0:NT * H],
                                                 0.0, None, ALU.not_equal), job)
                elif kind == "FLIP":
                    i = args[0]
                    wait_filled(dve, job)
                    drained_by(dve.tensor_copy(bias_near[:].rearrange("p h c -> p (h c)")[:, i * BANK:(i + 1) * BANK],
                                               bank_of(job)[:]), job)
                elif kind == "SEL":
                    b, i = args
                    wait_filled(dve, job)
                    if b > 0:
                        wait_filled(dve, ("T2", b - 1, 1))
                    ts = slice(i * NT // 2, (i + 1) * NT // 2)
                    drained_by(dve.tensor_tensor(gated[:, ts], bank_of(job)[:].rearrange("p (t d) -> p t d", d=D),
                                                 vu[:, b % 2, ts, D:], ALU.mult), job)
                elif kind == "LOG":
                    choose_experts(args[0], job)
                elif kind == "FF":
                    b, t, half = args
                    wait_filled(dve, job)
                    if NT * b + t >= 2 and half == 0:
                        dve.wait_ge(tile_done, NT * b + t - 1)
                    es = slice(half * E // 2, (half + 1) * E // 2)
                    drained_by(dve.tensor_tensor(ymix[:, t % 2, es], bank_of(job)[:].rearrange("p (e d) -> p e d", d=D),
                                                 gates[:, t, es].unsqueeze(2).to_broadcast([P, E // 2, D]), ALU.mult), job)

            def choose_experts(b, job):
                wide = lambda a: a.unsqueeze(2).to_broadcast([P, NT, E])
                wait_filled(dve, job)
                if b == 0:
                    dve.wait_ge(consts, 5 + QUADS + E)
                ins = dve.tensor_copy(lg[:, 0].rearrange("p t e -> p (t e)"), bank_of(job)[:, 0:NT * E])
                drained_by(ins, job)
                wait_drained(dve, job)
                for r in range(2):
                    then_wait(dve.tensor_reduce(top[:, r], lg[:, r], AX, ALU.max))
                    then_wait(dve.tensor_tensor(lg[:, 2], lg[:, r], wide(top[:, r]), ALU.is_equal))
                    then_wait(dve.tensor_tensor(lg[:, 2], lg[:, 2], rank[:].to_broadcast([P, NT, E]), ALU.mult))
                    then_wait(dve.tensor_reduce(top[:, 2 + r], lg[:, 2], AX, ALU.max))
                    then_wait(dve.tensor_tensor(pick[:, r], lg[:, 2], wide(top[:, 2 + r]), ALU.is_equal))
                    if r == 0:
                        then_wait(dve.scalar_tensor_tensor(lg[:, 1], pick[:, 0], -1e38, lg[:, 0], ALU.mult, ALU.add))
                dve.tensor_tensor(top[:, 4], top[:, 0], top[:, 1], ALU.subtract).then_inc(top_ready, 1)
                dve.wait_ge(tanh_ready, b + 1)
                then_wait(dve.tensor_scalar(gate2[:, 1], gate2[:, 0], -0.5, 0.5, ALU.mult, ALU.add))
                then_wait(dve.tensor_scalar(gate2[:, 0], gate2[:, 0], 0.5, 0.5, ALU.mult, ALU.add))
                for r in range(2):
                    then_wait(dve.tensor_tensor(pick[:, r], pick[:, r], wide(gate2[:, r]), ALU.mult))
                then_wait(dve.tensor_tensor(gates[:], pick[:, 0], pick[:, 1], ALU.add))

            then_wait(dve.memset(ext[:, 0:P - 1], NEG))
            then_wait(dve.memset(ext[:, P - 1 + MAXLEN:BANK], 0.0))
            dve.wait_ge(rb_in, 16)
            dve.tensor_scalar(ext[:, P - 1:P - 1 + MAXLEN], ext[:, BANK:BANK + MAXLEN],
                              ext[:, BANK + MAXLEN - 1:BANK + MAXLEN], None, ALU.subtract).then_inc(ext_ready, 1)
            dve.wait_ge(far_in, 16)
            dve.tensor_scalar(far[:], far_row[:], HD ** -0.5, None, ALU.mult).then_inc(far_ready, 1)

            for i, (group, jobs) in enumerate(TIMELINE):
                if i > 0 and TIMELINE[i - 1][0]:
                    for job in TIMELINE[i - 1][1]:
                        job_dve(job)
                    copy_outputs(TIMELINE[i - 1][0])
                if not group:
                    for job in jobs:
                        job_dve(job)
                if i + 1 < len(TIMELINE) and TIMELINE[i + 1][0]:
                    add_bias(TIMELINE[i + 1][0])


SCALES = [(j[1], int(j[0] == "stats2")) for _, jobs in TIMELINE for j in jobs if j[0] in ("stats1", "stats2")]
BIASED = {}
for _b in range(B):
    for _quad in range(QUADS):
        for _g, (_kb, _q0, _n) in enumerate(GROUPS):
            if _kb * P + NEAR > _q0:
                BIASED[order(_b, _quad, _g)] = len(BIASED)

_INS = ["L0_attn_x", "L0_attn_Wq", "L0_attn_Wk", "L0_attn_Wv", "L0_attn_Wu", "L0_attn_rel_bias",
        "L0_ffn_w_gate", "L0_ffn_w_in", "L0_ffn_w_out"]


def kernel(**inputs):
    import numpy as _np
    import concourse.bacc as _bacc
    from concourse import mybir as _mybir
    from concourse.bass_utils import run_bass_kernel_spmd as _run

    nc = _bacc.Bacc("TRN2", target_bir_lowering=False, num_devices=1)
    arrays, args = {}, []
    for name in _INS:
        a = _np.ascontiguousarray(inputs[name])
        arrays[f"in_{name}"] = a
        args.append(nc.dram_tensor(f"in_{name}", a.shape, _mybir.dt.from_np(a.dtype), kind="ExternalInput").ap())
    out = nc.dram_tensor("out_0", [B, S, D], _mybir.dt.float32, kind="ExternalOutput").ap()
    build(nc, *args, out)
    r = _run(nc, [arrays], core_ids=[0])
    return r.results[0]["out_0"]
```

```python
from contextlib import ExitStack

import concourse.bass as bass
from concourse import mybir

P = 128
B, S, D = 4, 1024, 128
H, HD = 8, 16
E, HID = 8, 512
MAXLEN = 256
NEG = -4294967295.0
EPS = 1e-5
NT = S // P
QUADS = H // 4
BANK = 512
NEAR = P + MAXLEN
HC = HID // P

F32 = mybir.dt.float32
F32R = mybir.dt.float32r
BF16 = mybir.dt.bfloat16
ALU = mybir.AluOpType
ACT = mybir.ActivationFunctionType
AX = mybir.AxisListType.X

HALF = S // 2
HT = NT // 2
GROUPS = [[(kb, max(kb * P, half * HALF), (half + 1) * HALF - max(kb * P, half * HALF)) for kb in range((half + 1) * HT)]
          for half in range(2)]
ORDER = [(b, half, quad, g) for b in range(B) for half in range(2) for quad in range(QUADS)
         for g in range(len(GROUPS[half]))]
INDEX = {group: n for n, group in enumerate(ORDER)}
ROW_PARTS = (2, 3)
STACK_DMAS = 2 * 2 * 2
BANKED = ("T1", "Q", "K", "VU", "MASK", "SEL", "T2", "LOG", "FF", "WT", "M", "FLIP")


PROJECT_FROM = (4, 15)
VU_FROM = (10, 24)


def unit_end(b, half):
    return INDEX[b, half, QUADS - 1, len(GROUPS[half]) - 1] + 1


def plan_timeline():
    beside = [[] for _ in ORDER]
    tail = []

    def put(slot, *jobs):
        for job in jobs:
            while job[0] in BANKED and slot < len(ORDER) and sum(j[0] in BANKED for j in beside[slot]) >= 2:
                slot += 1
            if slot >= len(ORDER):
                tail.append(job)
            else:
                beside[slot].append(job)
        first = slot < len(ORDER) and job in first_job(beside[slot])
        return slot + (1 if first else 2)

    def project(b, half, slot, vu_from):
        if b > 0:
            at = put(slot, ("stats1", b, half))
            at = put(at, ("norm1", b, half))
        else:
            at = slot
        at = put(at, ("T1", b, half))
        put(at, ("Q", b, half))
        at = put(at, ("K", b, half))
        at = put(at, ("split", b, half)) - 1
        at = max(at, vu_from)
        at = put(at, ("VU", b, 2 * half))
        at = put(at, ("VU", b, 2 * half + 1))
        put(at, ("MASK", b, half))

    def finish(b, half, slot, experts_from):
        at = put(slot, ("SEL", b, half))
        at = put(at, ("stats2", b, half))
        at = put(at, ("norm2", b, half))
        at = put(at, ("T2", b, half))
        at = put(at, ("LOG", b, half))
        put(at, ("best", b, half, 0))
        put(at + 1, ("best", b, half, 1))
        put(at + 2, ("gates", b, half))
        at = max(at + 3, experts_from)
        for t in range(half * HT, (half + 1) * HT):
            put(at, ("FF", b, t, 0))
            at = put(at, ("FF", b, t, 1)) - 1

    per = len(ORDER) // B
    experts_from = 0
    for b in range(B):
        s0 = b * per
        if b == 0:
            project(0, 1, 0, 0)
            for e in range(0, E, 2):
                experts_from = put(put(5 + 3 * (e // 2), ("WT", e), ("WT", e + 1)), ("M", e), ("M", e + 1))
        if b > 0:
            finish(b - 1, 1, s0 + 1, 0)
        if b + 1 < B:
            project(b + 1, 0, s0 + PROJECT_FROM[0], s0 + VU_FROM[0])
            project(b + 1, 1, s0 + PROJECT_FROM[1], s0 + VU_FROM[1])
        finish(b, 0, s0 + 9, experts_from)
    n = B - 1
    slots = [(None, [("stats1", 0, 0)]), (None, [("norm1", 0, 0)]), (None, [("T1", 0, 0)]),
             (None, [("Q", 0, 0), ("K", 0, 0), ("split", 0, 0), ("stats1", 0, 1), ("norm1", 0, 1)]),
             (None, [("VU", 0, 0), ("VU", 0, 1), ("MASK", 0, 0)] + [("FLIP", i) for i in range(H * NEAR // BANK)])]
    slots += list(zip(ORDER, beside))
    slots += [(None, tail), (None, [("SEL", n, 1)]), (None, [("stats2", n, 1)]), (None, [("norm2", n, 1)]),
              (None, [("T2", n, 1)]), (None, [("LOG", n, 1)]), (None, [("best", n, 1, 0)]), (None, [("best", n, 1, 1)]),
              (None, [("gates", n, 1)]), (None, [("FF", n, t, part) for t in range(HT, NT) for part in range(2)])]
    return slots


def first_job(jobs):
    return [j for j in jobs if j[0] in BANKED][:1]


def later_jobs(jobs):
    return [j for j in jobs if j not in first_job(jobs)]


TIMELINE = plan_timeline()
PROLOGUE = [group is None for group, _ in TIMELINE].index(False)
NUMBER = {}
for _group, _jobs in TIMELINE:
    for _j in _jobs:
        if _j[0] in BANKED:
            NUMBER[_j] = len(NUMBER)


def build(nc, x, Wq, Wk, Wv, Wu, rel_bias, w_gate, w_in, w_out, out):
    with ExitStack() as ctx:
        def sb(name, shape, dt=F32):
            return ctx.enter_context(nc.sbuf_tensor(name, shape, dt))

        def sem(name):
            return ctx.enter_context(nc.semaphore(name))

        xs = sb("xs", [P, B, NT, D])
        xn1 = sb("xn1", [P, NT, D])
        xn1T = sb("xn1T", [P, S])
        xn2 = sb("xn2", [P, NT, D])
        xn2T = sb("xn2T", [P, S])
        qk32 = [sb("q32", [P, S]), sb("k32", [P, S])]
        hi = [sb("q_hi", [P, S], F32R), sb("k_hi", [P, S], F32R)]
        lo = [sb("q_lo", [P, S], F32R), sb("k_lo", [P, S], F32R)]
        kabs = sb("kabs", [P, S], BF16)
        q_stack = sb("q_stack", [P, 2, H // 2, HALF], F32R)
        k_stack = sb("k_stack", [P, 2, H // 2, S], F32R)
        vu = sb("vu", [P, 2, NT, 2 * D])
        v_pad = sb("v_pad", [P, 2, NT, H, 32])
        kmask = sb("kmask", [P, NT, H])
        wts = sb("wts", [P, 2, 4, BANK])
        bias_rev = wts[:].rearrange("p a j c -> p (a j c)")[:, 0:H * NEAR]
        oT = sb("oT", [P, S])
        gated = xn2
        bias_near = sb("bias_near", [P, H, NEAR])
        far_row = sb("far_row", [P, H])
        far = sb("far", [P, H])
        ext = sb("ext", [H, BANK + MAXLEN])
        mm_e = sb("mm_e", [P, E, D])
        win_s = sb("win_s", [P, 2, HC, D])
        wout_s = sb("wout_s", [P, 2, HID])
        woutT = sb("woutT", [P, 2, HC, D])
        wq_s, wk_s, wvu_s = sb("wq_s", [P, D]), sb("wk_s", [P, D]), sb("wvu_s", [P, 2 * D])
        wg_s = sb("wg_s", [P, E])
        ident = sb("ident", [P, P])
        flip = sb("flip", [P, P])
        sel = sb("sel", [P, QUADS, 4, HD])
        headsum = sb("headsum", [P, H], BF16)
        stats = sb("stats", [P, 2, NT, 6])
        mv = sb("mv", [P, 2, NT, 2])
        rstd = sb("rstd", [P, 2, NT])
        eps_t = sb("eps_t", [P, NT])
        mhalf = sb("mhalf", [P, NT])
        rank = sb("rank", [P, 1, E])
        table_in = sb("table_in", [P, 1])
        lg = sb("lg", [P, 3, NT, E])
        pick = sb("pick", [P, 2, NT, E])
        top = sb("top", [P, 5, NT])
        gate2 = sb("gate2", [P, 2, NT])
        gates = sb("gates", [P, NT, E])
        ymix = sb("ymix", [P, 2, E, D])
        rows_dram = nc.dram_tensor("rows_dram", [2, 2, H, 3 * HD, S], F32, kind="Internal").ap()
        bias_dram = nc.dram_tensor("bias_dram", [H, BANK], F32, kind="Internal").ap()

        score = [ctx.enter_context(nc.psum_tensor(f"score{j}", [P, BANK], F32)) for j in range(4)]
        o_acc = [ctx.enter_context(nc.psum_tensor(f"o_acc{j}", [P, BANK], F32)) for j in range(2)]
        jobp = [ctx.enter_context(nc.psum_tensor(f"jobp{j}", [P, BANK], F32)) for j in range(2)]

        x_in = [[sem(f"x_in{b}_{half}") for half in range(2)] for b in range(B)]
        w_qk_in, w_vu_in, w_g_in = sem("w_qk_in"), sem("w_vu_in"), sem("w_g_in")
        rb_in, far_in, ext_out, bias_in = sem("rb_in"), sem("far_in"), sem("ext_out"), sem("bias_in")
        win_in = [sem(f"win_in{i}") for i in range(2)]
        wout_in = [sem(f"wout_in{i}") for i in range(2)]
        rows_out = [[sem(f"{side}_rows_out{half}") for half in range(2)] for side in "qk"]
        stack_in = [sem(f"stack_in{half}") for half in range(2)]
        stored = sem("stored")
        consts = sem("consts")
        zeroed = sem("zeroed")
        ext_set, ext_ready, far_ready = sem("ext_set"), sem("ext_ready"), sem("far_ready")
        averaged = sem("averaged")
        scaled = sem("scaled")
        normed1, normed2 = sem("normed1"), sem("normed2")
        filled = sem("filled")
        drained = [sem(f"drained{i}") for i in range(2)]
        kabs_ready = sem("kabs_ready")
        hi_ready, lo_ready = sem("hi_ready"), sem("lo_ready")
        v_ready = sem("v_ready")
        scored = [sem(f"scored{j}") for j in range(4)]
        biased = [sem(f"biased{j}") for j in range(4)]
        weighed = [sem(f"weighed{j}") for j in range(4)]
        pv_done = sem("pv_done")
        o_copied = [sem(f"o_copied{i}") for i in range(2)]
        x1_ready = sem("x1_ready")
        top_ready, tanh_ready, gates_ready = sem("top_ready"), sem("tanh_ready"), sem("gates_ready")
        tile_done = sem("tile_done")
        dve_step, pool_step = sem("dve_step"), sem("pool_step")

        def wait_filled(eng, job):
            eng.wait_ge(filled, NUMBER[job] + 1)

        def wait_drained(eng, job):
            n = NUMBER[job]
            eng.wait_ge(drained[n % 2], n // 2 + 1)

        def bank_of(job):
            return jobp[NUMBER[job] % 2]

        def drained_by(ins, job):
            ins.then_inc(drained[NUMBER[job] % 2], 1)

        block = ctx.enter_context(nc.Block())

        @block.sync
        def _(sp):
            def load_x(b, half):
                ts = slice(half * HT, (half + 1) * HT)
                sp.dma_start(xs[:, b, ts], x[b].rearrange("(t p) d -> p t d", p=P)[:, ts]).then_inc(x_in[b][half], 16)

            def load_expert(e):
                if e >= 2:
                    wait_filled(sp, ("M", e - 2))
                sp.dma_start(win_s[:, e % 2], w_in[e].rearrange("(c p) d -> p c d", p=P)).then_inc(win_in[e % 2], 16)
                sp.dma_start(wout_s[:, e % 2], w_out[e]).then_inc(wout_in[e % 2], 16)

            def write_rows(b, half, side):
                sp.wait_ge(hi_ready, 2 * (2 * b + half) + side + 1)
                sp.wait_ge(lo_ready, 2 * (2 * b + half) + side + 1)
                if b >= 2:
                    sp.wait_ge(stack_in[half], 16 * STACK_DMAS * (b - 1))
                cols = slice(half * HALF, (half + 1) * HALF)
                for k, part in enumerate((hi, lo, hi)[:ROW_PARTS[side]]):
                    sp.dma_start(rows_dram[b % 2, side, :, k * HD:(k + 1) * HD, cols], part[side][:, cols].bitcast(F32))\
                        .then_inc(rows_out[side][half], 16)

            def load_stack(b, half):
                cols = slice(half * HALF, (half + 1) * HALF)
                if b > 0:
                    for j in range(4):
                        sp.wait_ge(scored[j], unit_end(b - 1, half))
                for side, stack in ((0, q_stack[:, half]), (1, k_stack[:, b % 2, :, cols])):
                    sp.wait_ge(rows_out[side][half], 16 * ROW_PARTS[side] * (b + 1))
                    for odd in range(2):
                        for k in range(2):
                            first = k * HD if side else 0
                            row = 64 * odd + 32 * k
                            sp.dma_start(stack[row:row + 32].bitcast(F32),
                                         rows_dram[b % 2, side, odd::2, first:first + 32, cols]
                                         .rearrange("h r s -> r h s")).then_inc(stack_in[half], 16)

            def load_unit(b, half):
                write_rows(b, half, 0)
                write_rows(b, half, 1)
                load_stack(b, half)

            def store(b, half):
                sp.wait_ge(tile_done, NT * b + HT * (half + 1))
                ts = slice(half * HT, (half + 1) * HT)
                sp.dma_start(out[b].rearrange("(t p) d -> p t d", p=P)[:, ts], xs[:, b, ts]).then_inc(stored, 16)

            load_x(0, 0)
            sp.dma_start(wq_s[:], Wq).then_inc(w_qk_in, 16)
            sp.dma_start(wk_s[:], Wk).then_inc(w_qk_in, 16)
            sp.dma_start(ext[:, BANK:BANK + MAXLEN], rel_bias[MAXLEN - 1:, :].rearrange("r h -> h r"),
                         allow_slow_non_contiguous=True).then_inc(rb_in, 16)
            sp.dma_start(far_row[:], rel_bias[2 * MAXLEN - 2:, :].to_broadcast([P, H])).then_inc(far_in, 16)
            sp.dma_start(wvu_s[:, 0:D], Wv).then_inc(w_vu_in, 16)
            sp.dma_start(wvu_s[:, D:], Wu).then_inc(w_vu_in, 16)
            sp.dma_start(wg_s[:], w_gate.rearrange("e d -> d e"), allow_slow_non_contiguous=True).then_inc(w_g_in, 16)
            sp.wait_ge(ext_ready, 1)
            sp.dma_start(bias_dram, ext[:, 0:BANK]).then_inc(ext_out, 16)
            sp.wait_ge(ext_out, 16)
            sp.dma_start(bias_rev.rearrange("p (h c) -> p h c", h=H),
                         bass.AP(bias_dram.tensor, 0, [[1, P], [BANK, H], [1, NEAR]])).then_inc(bias_in, 16)
            load_x(0, 1)
            load_unit(0, 0)
            load_expert(0)
            load_expert(1)
            load_unit(0, 1)
            for b in range(1, B):
                load_x(b, 0)
                load_x(b, 1)
            for e in range(2, E):
                load_expert(e)
            for b in range(1, B):
                load_unit(b, 0)
                if b > 1:
                    store(b - 2, 1)
                load_unit(b, 1)
                store(b - 1, 0)
            store(B - 2, 1)
            store(B - 1, 0)
            store(B - 1, 1)
            sp.wait_ge(stored, 16 * 2 * B)

        @block.gpsimd
        def _(pool):
            step = [0]

            def then_wait(ins):
                step[0] += 1
                ins.then_inc(pool_step, 1)
                pool.wait_ge(pool_step, step[0])

            def scale(unit, ln):
                n = SCALES.index((unit, ln))
                pool.wait_ge(averaged, n + 1)
                if unit[0] > 0:
                    pool.wait_ge((normed1, normed2)[ln], 2 * (unit[0] - 1) + unit[1] + 1)
                ts = slice(unit[1] * HT, (unit[1] + 1) * HT)
                then_wait(pool.tensor_tensor(rstd[:, ln, ts], mv[:, ln, ts, 1], eps_t[:, ts], ALU.add))
                pool.tensor_tensor(rstd[:, ln, ts], rstd[:, ln, ts], mhalf[:, ts], ALU.pow).then_inc(scaled, 1)

            pool.memset(eps_t[:], EPS).then_inc(consts, 1)
            pool.memset(mhalf[:], -0.5).then_inc(consts, 1)
            then_wait(pool.memset(ident[:], 0.0))
            pool.affine_select(out=ident[:], in_=ident[:], compare_op=ALU.not_equal, fill=1.0, base=0,
                               pattern=[[-1, P]], channel_multiplier=1).then_inc(consts, 1)
            scale((0, 0), 0)
            pool.memset(v_pad[:], 0.0).then_inc(zeroed, 1)
            then_wait(pool.memset(headsum[:], 1.0))
            then_wait(pool.affine_select(out=headsum[:], in_=headsum[:], compare_op=ALU.is_ge, fill=0.0, base=0,
                                         pattern=[[-HD, H]], channel_multiplier=1))
            pool.affine_select(out=headsum[:], in_=headsum[:], compare_op=ALU.is_ge, fill=0.0, base=HD - 1,
                               pattern=[[HD, H]], channel_multiplier=-1).then_inc(consts, 1)
            then_wait(pool.memset(flip[:], 0.0))
            pool.affine_select(out=flip[:], in_=flip[:], compare_op=ALU.not_equal, fill=1.0, base=1 - P,
                               pattern=[[1, P]], channel_multiplier=1).then_inc(consts, 1)
            then_wait(pool.memset(sel[:], 0.0))
            pool.affine_select(out=sel[:], in_=sel[:], compare_op=ALU.not_equal, fill=1.0, base=0,
                               pattern=[[-HD, QUADS], [-32, 4], [-1, HD]], channel_multiplier=1).then_inc(consts, 1)
            for e in range(E):
                pool.memset(rank[:, :, e:e + 1], float(E - e)).then_inc(consts, 1)

            def split_lo(b, half):
                cols = slice(half * HALF, (half + 1) * HALF)
                for side in range(2):
                    pool.wait_ge(hi_ready, 2 * (2 * b + half) + side + 1)
                    pool.tensor_tensor(lo[side][:, cols], qk32[side][:, cols], hi[side][:, cols].bitcast(F32),
                                       ALU.subtract).then_inc(lo_ready, 1)

            def mask_v(b, half):
                wait_drained(pool, ("MASK", b, half))
                wait_drained(pool, ("VU", b, 2 * half))
                wait_drained(pool, ("VU", b, 2 * half + 1))
                if b == 0 and half == 0:
                    pool.wait_ge(zeroed, 1)
                if b >= 2:
                    pool.wait_ge(pv_done, unit_end(b - 2, 1))
                ts = slice(half * HT, (half + 1) * HT)
                for quad in range(QUADS):
                    hs = slice(4 * quad, 4 * quad + 4)
                    pool.tensor_tensor(v_pad[:, b % 2, ts, hs, HD * quad:HD * quad + HD],
                                       vu[:, b % 2, ts, 4 * quad * HD:4 * (quad + 1) * HD].rearrange("p t (h d) -> p t h d", h=4),
                                       kmask[:, ts, hs].unsqueeze(3).to_broadcast([P, HT, 4, HD]), ALU.mult)\
                        .then_inc(v_ready, 1)

            def add_attention(b, half):
                wait_drained(pool, ("SEL", b, half))
                ts = slice(half * HT, (half + 1) * HT)
                pool.tensor_tensor(xs[:, b, ts], xs[:, b, ts], gated[:, ts], ALU.add).then_inc(x1_ready, 1)

            def add_experts(b, t):
                wait_drained(pool, ("FF", b, t, 0))
                wait_drained(pool, ("FF", b, t, 1))
                y = ymix[:, t % 2]
                n = E // 2
                while n >= 1:
                    then_wait(pool.tensor_tensor(y[:, 0:n], y[:, 0:n], y[:, n:2 * n], ALU.add))
                    n //= 2
                pool.tensor_tensor(xs[:, b, t], xs[:, b, t], y[:, 0], ALU.add).then_inc(tile_done, 1)

            def jobs(i):
                for job in TIMELINE[i][1]:
                    kind = job[0]
                    if kind in ("stats1", "stats2") and i > 0:
                        scale(job[1:], int(kind == "stats2"))
                    elif kind == "split" and i >= PROLOGUE:
                        split_lo(job[1], job[2])
                    elif kind == "MASK":
                        mask_v(job[1], job[2])
                    elif kind == "SEL":
                        add_attention(job[1], job[2])
                    elif kind == "FF" and job[3] == 1:
                        add_experts(job[1], job[2])

            for i in range(len(TIMELINE)):
                jobs(i)

        @block.tensor
        def _(pe):
            def scores(group, j):
                b, half, quad, g = group
                kb, q0, n = GROUPS[half][g]
                h = 4 * quad + j
                rows = slice(64 * (h % 2), 64 * (h % 2) + 64)
                if quad == 0 and g == 0 and j == 0:
                    pe.wait_ge(stack_in[half], 16 * STACK_DMAS * (b + 1))
                if INDEX[group] > 0:
                    pe.wait_ge(weighed[j], INDEX[group])
                pe.matmul(score[j][:, 0:n], k_stack[rows, b % 2, h // 2, kb * P:(kb + 1) * P],
                          q_stack[rows, half, h // 2, q0 - half * HALF:q0 - half * HALF + n],
                          start=True, stop=True).then_inc(scored[j], 1)

            def times_v(group):
                b, half, quad, g = group
                kb, q0, n = GROUPS[half][g]
                c0 = q0 - half * HALF
                if quad == 0 and g == 0:
                    pe.wait_ge(v_ready, QUADS * (2 * b + half + 1))
                    if b > 0:
                        pe.wait_ge(o_copied[half], b)
                for j in range(4):
                    pe.wait_ge(weighed[j], INDEX[group] + 1)
                for j in range(4):
                    ins = pe.matmul(o_acc[half][32 * j:32 * j + 32, c0:c0 + n], v_pad[:, b % 2, kb, 4 * quad + j, :],
                                    wts[:, INDEX[group] % 2, j, 0:n], start=(quad == 0 and g == 0),
                                    stop=(INDEX[group] + 1 == unit_end(b, half)))
                ins.then_inc(pv_done, 1)

            def job_pe(job):
                kind, args = job[0], job[1:]
                if kind not in BANKED:
                    return
                n = NUMBER[job]
                bank = jobp[n % 2]
                if n >= 2:
                    pe.wait_ge(drained[n % 2], n // 2)
                if kind in ("T1", "T2"):
                    b, half = args
                    src, ready = (xn1, normed1) if kind == "T1" else (xn2, normed2)
                    if n == 0:
                        pe.wait_ge(consts, 3)
                    pe.wait_ge(ready, 2 * b + half + 1)
                    for k in range(HT):
                        ins = pe.transpose(bank[:, k * P:(k + 1) * P], src[:, HT * half + k, :], ident[:])
                elif kind in ("Q", "K"):
                    b, half = args
                    pe.wait_ge(w_qk_in, 32)
                    wait_drained(pe, ("T1", b, half))
                    ins = pe.matmul(bank[:], (wq_s if kind == "Q" else wk_s)[:], xn1T[:, half * HALF:(half + 1) * HALF],
                                    start=True, stop=True)
                elif kind == "VU":
                    b, i = args
                    pe.wait_ge(w_vu_in, 32)
                    for k in range(2):
                        t = 2 * i + k
                        ins = pe.matmul(bank[:, k * 2 * D:(k + 1) * 2 * D], xn1T[:, t * P:(t + 1) * P], wvu_s[:],
                                        start=True, stop=True)
                elif kind == "MASK":
                    b, half = args
                    if b == 0 and half == 0:
                        pe.wait_ge(consts, 4)
                    pe.wait_ge(kabs_ready, 2 * b + half + 1)
                    for k in range(HT):
                        t = HT * half + k
                        ins = pe.matmul(bank[:, k * H:(k + 1) * H], kabs[:, t * P:(t + 1) * P], headsum[:],
                                        start=True, stop=True)
                elif kind == "SEL":
                    b, half = args
                    if b == 0 and half == 0:
                        pe.wait_ge(consts, 6)
                    pe.wait_ge(o_copied[half], b + 1)
                    for k in range(HT):
                        t = HT * half + k
                        ins = pe.matmul(bank[:, k * D:(k + 1) * D], oT[:, t * P:(t + 1) * P],
                                        sel[:].rearrange("p q j d -> p (q j d)"), start=True, stop=True)
                elif kind == "LOG":
                    b, half = args
                    pe.wait_ge(w_g_in, 16)
                    wait_drained(pe, ("T2", b, half))
                    for k in range(HT):
                        t = HT * half + k
                        ins = pe.matmul(bank[:, k * E:(k + 1) * E], xn2T[:, t * P:(t + 1) * P], wg_s[:],
                                        start=True, stop=True)
                elif kind == "FF":
                    b, t, part = args
                    if b == 0 and t == 0:
                        wait_drained(pe, ("M", E - 1))
                        wait_drained(pe, ("M", E - 2))
                    ins = pe.matmul(bank[:], xn2T[:, t * P:(t + 1) * P],
                                    mm_e[:, part * E // 2:(part + 1) * E // 2, :].rearrange("p e d -> p (e d)"),
                                    start=True, stop=True)
                elif kind == "FLIP":
                    i = args[0]
                    pe.wait_ge(bias_in, 16)
                    pe.wait_ge(consts, 5)
                    ins = pe.matmul(bank[:], flip[:], bias_rev[:, i * BANK:(i + 1) * BANK], start=True, stop=True)
                elif kind == "WT":
                    e = args[0]
                    pe.wait_ge(wout_in[e % 2], 16 * (e // 2 + 1))
                    for c in range(HC):
                        ins = pe.transpose(bank[:, c * P:(c + 1) * P], wout_s[:, e % 2, c * P:(c + 1) * P], ident[:])
                elif kind == "M":
                    e = args[0]
                    pe.wait_ge(win_in[e % 2], 16 * (e // 2 + 1))
                    wait_drained(pe, ("WT", e))
                    for c in range(HC):
                        ins = pe.matmul(bank[:, 0:D], win_s[:, e % 2, c, :], woutT[:, e % 2, c, :],
                                        start=(c == 0), stop=(c == HC - 1))
                ins.then_inc(filled, 1)

            for i, (group, jobs) in enumerate(TIMELINE):
                before = TIMELINE[i - 1][0] if i > 0 else None
                after = TIMELINE[i + 1][0] if i + 1 < len(TIMELINE) else None
                if group and after:
                    scores(after, 0)
                if before:
                    times_v(before)
                if group and after:
                    scores(after, 1)
                for job in first_job(jobs):
                    job_pe(job)
                if group and after:
                    scores(after, 2)
                for job in later_jobs(jobs):
                    job_pe(job)
                if group and after:
                    scores(after, 3)
                if after and not group:
                    for j in range(4):
                        scores(after, j)

        @block.scalar
        def _(act):
            def weigh(group, j):
                b, half, quad, g = group
                kb, q0, n = GROUPS[half][g]
                number = INDEX[group]
                if number == 0 and j == 0:
                    act.wait_ge(far_ready, 1)
                if group in BIASED:
                    act.wait_ge(biased[j], BIASED[group] + 1)
                else:
                    act.wait_ge(scored[j], number + 1)
                if number >= 2 and j == 0:
                    act.wait_ge(pv_done, number - 1)
                h = 4 * quad + j
                act.activation(wts[:, number % 2, j, 0:n], score[j][:, 0:n], ACT.Silu,
                               bias=far[:, h:h + 1], scale=HD ** -0.5).then_inc(weighed[j], 1)

            def job_act(job):
                kind, args = job[0], job[1:]
                if kind in ("T1", "T2"):
                    b, half = args
                    dst = xn1T if kind == "T1" else xn2T
                    wait_filled(act, job)
                    if b > 0:
                        wait_filled(act, ("VU", b - 1, 2 * half + 1) if kind == "T1" else ("FF", b - 1, HT * (half + 1) - 1, 1))
                    drained_by(act.copy(dst[:, half * HALF:(half + 1) * HALF], bank_of(job)[:]), job)
                elif kind in ("Q", "K"):
                    b, half = args
                    side = int(kind == "K")
                    wait_filled(act, job)
                    if b > 0:
                        act.wait_ge(lo_ready, 2 * (2 * (b - 1) + half) + side + 1)
                        if side:
                            wait_filled(act, ("MASK", b - 1, half))
                    cols = slice(half * HALF, (half + 1) * HALF)
                    drained_by(act.activation(qk32[side][:, cols], bank_of(job)[:], ACT.Silu), job)
                    if side:
                        wait_drained(act, job)
                        act.activation(kabs[:, cols], qk32[1][:, cols], ACT.Abs).then_inc(kabs_ready, 1)
                elif kind == "VU":
                    b, i = args
                    wait_filled(act, job)
                    if b >= 2:
                        act.wait_ge(v_ready, QUADS * (2 * (b - 2) + i // 2 + 1))
                        wait_drained(act, ("SEL", b - 2, i // 2))
                    drained_by(act.activation(vu[:, b % 2, 2 * i:2 * i + 2, :].rearrange("p t d -> p (t d)"),
                                              bank_of(job)[:], ACT.Silu), job)
                elif kind == "gates":
                    b, half = args
                    ts = slice(half * HT, (half + 1) * HT)
                    act.wait_ge(top_ready, 2 * b + half + 1)
                    act.activation(gate2[:, 0, ts], top[:, 4, ts], ACT.Tanh, scale=0.5).then_inc(tanh_ready, 1)
                elif kind == "WT":
                    e = args[0]
                    wait_filled(act, job)
                    if e >= 2:
                        wait_filled(act, ("M", e - 2))
                    drained_by(act.copy(woutT[:, e % 2].rearrange("p c d -> p (c d)"), bank_of(job)[:]), job)
                elif kind == "M":
                    wait_filled(act, job)
                    drained_by(act.copy(mm_e[:, args[0], :], bank_of(job)[:, 0:D]), job)

            act.wait_ge(consts, 1)
            act.activation(table_in[:], eps_t[:, 0:1], ACT.Silu)
            for i, (group, jobs) in enumerate(TIMELINE):
                if group:
                    weigh(group, 0)
                if i > 0 and TIMELINE[i - 1][0]:
                    for job in later_jobs(TIMELINE[i - 1][1]):
                        job_act(job)
                if group:
                    weigh(group, 1)
                    weigh(group, 2)
                    weigh(group, 3)
                    for job in first_job(jobs):
                        job_act(job)
                else:
                    for job in jobs:
                        job_act(job)

        @block.vector
        def _(dve):
            step = [0]

            def then_wait(ins):
                step[0] += 1
                ins.then_inc(dve_step, 1)
                dve.wait_ge(dve_step, step[0])

            def add_bias(group, j):
                b, half, quad, g = group
                kb, q0, n = GROUPS[half][g]
                if group not in BIASED:
                    return
                c0 = q0 - kb * P
                near = min(n, NEAR - c0)
                if INDEX[group] == 0:
                    for i in range(2):
                        wait_drained(dve, ("FLIP", H * NEAR // BANK - 1 - i))
                dve.wait_ge(scored[j], INDEX[group] + 1)
                dve.tensor_tensor(score[j][:, 0:near], score[j][:, 0:near], bias_near[:, 4 * quad + j, c0:c0 + near],
                                  ALU.add).then_inc(biased[j], 1)

            def copy_outputs(group):
                b, half, quad, g = group
                if INDEX[group] + 1 != unit_end(b, half):
                    return
                dve.wait_ge(pv_done, INDEX[group] + 1)
                if b > 0:
                    wait_filled(dve, ("SEL", b - 1, half))
                dve.tensor_copy(oT[:, half * HALF:(half + 1) * HALF], o_acc[half][:]).then_inc(o_copied[half], 1)

            def job_dve(job):
                kind, args = job[0], job[1:]
                if kind in ("stats1", "stats2"):
                    b, half = args
                    ln = int(kind == "stats2")
                    if ln:
                        dve.wait_ge(x1_ready, 2 * b + half + 1)
                    else:
                        dve.wait_ge(x_in[b][half], 16)
                    for t in range(HT * half, HT * (half + 1)):
                        ins = dve.bn_stats(stats[:, ln, t, :], xs[:, b, t, :])
                    then_wait(ins)
                    for t in range(HT * half, HT * (half + 1)):
                        ins = dve.bn_aggr(mv[:, ln, t, :], stats[:, ln, t, :])
                    ins.then_inc(averaged, 1)
                elif kind in ("norm1", "norm2"):
                    b, half = args
                    ln = int(kind == "norm2")
                    dve.wait_ge(scaled, SCALES.index((args, ln)) + 1)
                    if b > 0:
                        wait_filled(dve, (("T1", "T2")[ln], b - 1, half))
                    dst = xn2 if ln else xn1
                    for t in range(HT * half, HT * (half + 1)):
                        ins = dve.tensor_scalar(dst[:, t, :], xs[:, b, t, :], mv[:, ln, t, 0:1], rstd[:, ln, t:t + 1],
                                                ALU.subtract, ALU.mult)
                    ins.then_inc((normed1, normed2)[ln], 1)
                elif kind == "split":
                    b, half = args
                    cols = slice(half * HALF, (half + 1) * HALF)
                    for side in range(2):
                        if b > 0:
                            dve.wait_ge(rows_out[side][half], 16 * ROW_PARTS[side] * b)
                        wait_drained(dve, ("QK"[side], b, half))
                        ins = dve.tensor_copy(hi[side][:, cols], qk32[side][:, cols])
                        ins.then_inc(hi_ready, 1)
                        if b == 0 and half == 0:
                            dve.wait_ge(hi_ready, side + 1)
                            dve.tensor_tensor(lo[side][:, cols], qk32[side][:, cols], hi[side][:, cols].bitcast(F32),
                                              ALU.subtract).then_inc(lo_ready, 1)
                elif kind == "MASK":
                    b, half = args
                    wait_filled(dve, job)
                    if b > 0:
                        dve.wait_ge(v_ready, QUADS * (2 * (b - 1) + half + 1))
                    ts = slice(half * HT, (half + 1) * HT)
                    drained_by(dve.tensor_scalar(kmask[:, ts].rearrange("p t h -> p (t h)"), bank_of(job)[:, 0:HT * H],
                                                 0.0, None, ALU.not_equal), job)
                elif kind == "FLIP":
                    i = args[0]
                    wait_filled(dve, job)
                    drained_by(dve.tensor_copy(bias_near[:].rearrange("p h c -> p (h c)")[:, i * BANK:(i + 1) * BANK],
                                               bank_of(job)[:]), job)
                elif kind == "SEL":
                    b, half = args
                    wait_filled(dve, job)
                    if b > 0:
                        wait_filled(dve, ("T2", b - 1, half))
                    ts = slice(half * HT, (half + 1) * HT)
                    drained_by(dve.tensor_tensor(gated[:, ts], bank_of(job)[:].rearrange("p (t d) -> p t d", d=D),
                                                 vu[:, b % 2, ts, D:], ALU.mult), job)
                elif kind == "LOG":
                    b, half = args
                    wait_filled(dve, job)
                    ts = slice(half * HT, (half + 1) * HT)
                    drained_by(dve.tensor_copy(lg[:, 0, ts].rearrange("p t e -> p (t e)"), bank_of(job)[:, 0:HT * E]), job)
                elif kind == "best":
                    take_best(*args)
                elif kind == "gates":
                    mix_gates(*args)
                elif kind == "FF":
                    b, t, part = args
                    wait_filled(dve, job)
                    if NT * b + t >= 2 and part == 0:
                        dve.wait_ge(tile_done, NT * b + t - 1)
                    es = slice(part * E // 2, (part + 1) * E // 2)
                    drained_by(dve.tensor_tensor(ymix[:, t % 2, es], bank_of(job)[:].rearrange("p (e d) -> p e d", d=D),
                                                 gates[:, t, es].unsqueeze(2).to_broadcast([P, E // 2, D]), ALU.mult), job)

            def wide(a):
                return a.unsqueeze(2).to_broadcast([P, HT, E])

            def take_best(b, half, r):
                ts = slice(half * HT, (half + 1) * HT)
                if r == 0:
                    wait_drained(dve, ("LOG", b, half))
                if r == 0 and b == 0 and half == 0:
                    dve.wait_ge(consts, 6 + E)
                if r == 1:
                    then_wait(dve.scalar_tensor_tensor(lg[:, 1, ts], pick[:, 0, ts], -1e38, lg[:, 0, ts], ALU.mult, ALU.add))
                then_wait(dve.tensor_reduce(top[:, r, ts], lg[:, r, ts], AX, ALU.max))
                then_wait(dve.tensor_tensor(lg[:, 2, ts], lg[:, r, ts], wide(top[:, r, ts]), ALU.is_equal))
                then_wait(dve.tensor_tensor(lg[:, 2, ts], lg[:, 2, ts], rank[:].to_broadcast([P, HT, E]), ALU.mult))
                then_wait(dve.tensor_reduce(top[:, 2 + r, ts], lg[:, 2, ts], AX, ALU.max))
                then_wait(dve.tensor_tensor(pick[:, r, ts], lg[:, 2, ts], wide(top[:, 2 + r, ts]), ALU.is_equal))
                if r == 1:
                    dve.tensor_tensor(top[:, 4, ts], top[:, 0, ts], top[:, 1, ts], ALU.subtract).then_inc(top_ready, 1)

            def mix_gates(b, half):
                ts = slice(half * HT, (half + 1) * HT)
                dve.wait_ge(tanh_ready, 2 * b + half + 1)
                then_wait(dve.tensor_scalar(gate2[:, 1, ts], gate2[:, 0, ts], -0.5, 0.5, ALU.mult, ALU.add))
                then_wait(dve.tensor_scalar(gate2[:, 0, ts], gate2[:, 0, ts], 0.5, 0.5, ALU.mult, ALU.add))
                for r in range(2):
                    then_wait(dve.tensor_tensor(pick[:, r, ts], pick[:, r, ts], wide(gate2[:, r, ts]), ALU.mult))
                then_wait(dve.tensor_tensor(gates[:, ts], pick[:, 0, ts], pick[:, 1, ts], ALU.add))

            def set_biases():
                then_wait(dve.memset(ext[:, 0:P - 1], NEG))
                then_wait(dve.memset(ext[:, P - 1 + MAXLEN:BANK], 0.0))
                dve.wait_ge(rb_in, 16)
                dve.tensor_scalar(ext[:, P - 1:P - 1 + MAXLEN], ext[:, BANK:BANK + MAXLEN],
                                  ext[:, BANK + MAXLEN - 1:BANK + MAXLEN], None, ALU.subtract).then_inc(ext_ready, 1)
                dve.wait_ge(far_in, 16)
                dve.tensor_scalar(far[:], far_row[:], HD ** -0.5, None, ALU.mult).then_inc(far_ready, 1)

            for i, (group, jobs) in enumerate(TIMELINE):
                before = TIMELINE[i - 1][0] if i > 0 else None
                after = TIMELINE[i + 1][0] if i + 1 < len(TIMELINE) else None
                if not group:
                    if before:
                        for job in later_jobs(TIMELINE[i - 1][1]):
                            job_dve(job)
                        copy_outputs(before)
                    for job in jobs:
                        job_dve(job)
                    if i == 0:
                        set_biases()
                if after:
                    add_bias(after, 0)
                if group and before:
                    for job in later_jobs(TIMELINE[i - 1][1]):
                        job_dve(job)
                if after:
                    add_bias(after, 1)
                if group:
                    for job in first_job(jobs):
                        job_dve(job)
                if after:
                    add_bias(after, 2)
                    add_bias(after, 3)
                if group and before:
                    copy_outputs(before)


SCALES = [(j[1:], int(j[0] == "stats2")) for _, jobs in TIMELINE for j in jobs if j[0] in ("stats1", "stats2")]
BIASED = {}
for _group in ORDER:
    _kb, _q0, _n = GROUPS[_group[1]][_group[3]]
    if _kb * P + NEAR > _q0:
        BIASED[_group] = len(BIASED)

_INS = ["L0_attn_x", "L0_attn_Wq", "L0_attn_Wk", "L0_attn_Wv", "L0_attn_Wu", "L0_attn_rel_bias",
        "L0_ffn_w_gate", "L0_ffn_w_in", "L0_ffn_w_out"]


def kernel(**inputs):
    import numpy as _np
    import concourse.bacc as _bacc
    from concourse import mybir as _mybir
    from concourse.bass_utils import run_bass_kernel_spmd as _run

    nc = _bacc.Bacc("TRN2", target_bir_lowering=False, num_devices=1)
    arrays, args = {}, []
    for name in _INS:
        a = _np.ascontiguousarray(inputs[name])
        arrays[f"in_{name}"] = a
        args.append(nc.dram_tensor(f"in_{name}", a.shape, _mybir.dt.from_np(a.dtype), kind="ExternalInput").ap())
    out = nc.dram_tensor("out_0", [B, S, D], _mybir.dt.float32, kind="ExternalOutput").ap()
    build(nc, *args, out)
    r = _run(nc, [arrays], core_ids=[0])
    return r.results[0]["out_0"]
```

```python
from contextlib import ExitStack

import concourse.bass as bass
from concourse import mybir

P = 128
B, S, D = 4, 1024, 128
H, HD = 8, 16
E, HID = 8, 512
MAXLEN = 256
NEG = -4294967295.0
EPS = 1e-5
NT = S // P
QUADS = H // 4
BANK = 512
NEAR = P + MAXLEN
HC = HID // P
FLIPS = H * NEAR // BANK

F32 = mybir.dt.float32
F32R = mybir.dt.float32r
BF16 = mybir.dt.bfloat16
ALU = mybir.AluOpType
ACT = mybir.ActivationFunctionType
AX = mybir.AxisListType.X

HALF = S // 2
HT = NT // 2
GROUPS = [[(kb, max(kb * P, half * HALF), (half + 1) * HALF - max(kb * P, half * HALF)) for kb in range((half + 1) * HT)]
          for half in range(2)]
ORDER = [(b, half, quad, g) for b in range(B) for half in range(2) for quad in range(QUADS)
         for g in range(len(GROUPS[half]))]
INDEX = {group: n for n, group in enumerate(ORDER)}
ROW_PARTS = (2, 3)
STACK_DMAS = 2 * 2 * 2
BANKED = ("T1", "Q", "K", "VU", "MASK", "SEL", "T2", "LOG", "FF", "WT", "M", "FLIP")


PROJECT_FROM = (4, 18)
VU_FROM = (10, 26)
EXPERTS_FROM, EXPERTS_STEP = 5, 5
ROOM = (2, 1, 2, 2)
LATER = {
    ("FF", 0, 1, 1): -1, ("FF", 0, 2, 1): 1, ("FF", 0, 7, 0): 1, ("FF", 1, 1, 1): -1,
    ("FF", 1, 7, 0): 1, ("FF", 2, 1, 1): -1, ("FF", 2, 7, 0): 1, ("FF", 2, 7, 1): 1, ("LOG", 2, 1): 1,
    ("M", 5): 1, ("MASK", 0, 1): -1, ("MASK", 1, 1): -1, ("MASK", 2, 1): -1, ("MASK", 3, 1): -1,
    ("T1", 1, 0): 1, ("VU", 0, 2): 1, ("VU", 0, 3): 1, ("VU", 1, 2): 1, ("VU", 1, 3): 1,
    ("VU", 2, 2): 1, ("VU", 2, 3): 1, ("VU", 3, 2): 1, ("VU", 3, 3): 1, ("norm2", 0, 0): 2,
    ("norm2", 1, 0): 2, ("norm2", 2, 0): 2, ("norm2", 3, 0): 2, ("split", 0, 1): -2, ("split", 1, 0): 1,
    ("split", 2, 0): 1, ("split", 3, 0): 1,
}


LAST_TILES = (HT, HT + 2, HT + 1, HT + 3)
ACT_SCALES = LAST_TILES[1::2]
POOL_SUMS = LAST_TILES[:2]


def unit_end(b, half):
    return INDEX[b, half, QUADS - 1, len(GROUPS[half]) - 1] + 1


def plan_timeline():
    beside = [[] for _ in ORDER]
    tail = []

    def put(slot, *jobs):
        for job in jobs:
            slot += LATER.get(job, 0)
            while job[0] in BANKED and slot < len(ORDER) and sum(j[0] in BANKED for j in beside[slot]) >= room(slot):
                slot += 1
            if slot >= len(ORDER):
                tail.append(job)
            else:
                beside[slot].append(job)
        first = slot < len(ORDER) and job in first_job(beside[slot])
        return slot + (1 if first else 2)

    def room(slot):
        b, half, quad, g = ORDER[slot]
        return ROOM[GROUPS[half][g][2] // P - 1]

    def project(b, half, slot, vu_from):
        if b > 0:
            at = put(slot, ("stats1", b, half))
            at = put(at, ("norm1", b, half))
        else:
            at = slot
        at = put(at, ("T1", b, half))
        put(at, ("Q", b, half))
        at = put(at, ("K", b, half))
        at = put(at, ("split", b, half)) - 1
        at = max(at, vu_from)
        at = put(at, ("VU", b, 2 * half))
        at = put(at, ("VU", b, 2 * half + 1))
        put(at, ("MASK", b, half))

    def finish(b, half, slot, experts_from):
        at = put(slot, ("SEL", b, half))
        at = put(at, ("stats2", b, half))
        at = put(at, ("norm2", b, half))
        at = put(at, ("T2", b, half))
        at = put(at, ("LOG", b, half))
        put(at, ("best", b, half, 0))
        put(at + 1, ("best", b, half, 1))
        put(at + 2, ("gates", b, half))
        at = max(at + 3, experts_from)
        for t in range(half * HT, (half + 1) * HT):
            if (b, t) not in ((B - 1, HT - 2), (B - 1, HT - 1)):
                put(at, ("FF", b, t, 0))
                at = put(at, ("FF", b, t, 1)) - 1

    per = len(ORDER) // B
    experts_from = 0
    for b in range(B):
        s0 = b * per
        if b == 0:
            project(0, 1, 0, 0)
            for e in range(2, E, 2):
                experts_from = put(put(EXPERTS_FROM + EXPERTS_STEP * (e // 2 - 1), ("WT", e), ("WT", e + 1)), ("M", e), ("M", e + 1))
        if b > 0:
            finish(b - 1, 1, s0 + 1, 0)
        if b + 1 < B:
            project(b + 1, 0, s0 + PROJECT_FROM[0], s0 + VU_FROM[0])
            project(b + 1, 1, s0 + PROJECT_FROM[1], s0 + VU_FROM[1])
        finish(b, 0, s0 + 9, experts_from)
    n = B - 1
    slots = [(None, [("stats1", 0, 0)]), (None, [("norm1", 0, 0)]), (None, [("T1", 0, 0)]),
             (None, [("Q", 0, 0), ("K", 0, 0), ("split", 0, 0), ("stats1", 0, 1)]),
             (None, [("VU", 0, 0), ("VU", 0, 1), ("MASK", 0, 0), ("WT", 0), ("WT", 1), ("FLIP", 0), ("M", 0),
                     ("FLIP", 1), ("M", 1), ("norm1", 0, 1)] + [("FLIP", i) for i in range(2, FLIPS)])]
    slots += list(zip(ORDER, beside))
    slots += [(None, tail), (None, [("SEL", n, 1)]), (None, [("stats2", n, 1)]),
              (None, [("FF", n, HT - 2, 0), ("FF", n, HT - 2, 1), ("norm2", n, 1), ("T2", n, 1)]),
              (None, [("LOG", n, 1)]), (None, [("best", n, 1, 0)]), (None, [("best", n, 1, 1)]),
              (None, [("FF", n, HT - 1, 0), ("FF", n, HT - 1, 1), ("gates", n, 1)]),
              (None, [("FF", n, t, part) for t in LAST_TILES for part in range(2)])]
    return slots


def first_job(jobs):
    return [j for j in jobs if j[0] in BANKED][:1]


def later_jobs(jobs):
    return [j for j in jobs if j not in first_job(jobs)]


TIMELINE = plan_timeline()
PROLOGUE = [group is None for group, _ in TIMELINE].index(False)
NUMBER = {j: n for n, j in enumerate(j for _, jobs in TIMELINE for j in jobs if j[0] in BANKED)}


def bank_use(job):
    n, shared = NUMBER[job], len(NUMBER) - 2 * HT
    if n < shared:
        return n % 2, n // 2
    if n < shared + 6:
        return 2 + n - shared, 0
    return (n - 6) % 2, (n - 6) // 2


def build(nc, x, Wq, Wk, Wv, Wu, rel_bias, w_gate, w_in, w_out, out):
    with ExitStack() as ctx:
        def sb(name, shape, dt=F32):
            return ctx.enter_context(nc.sbuf_tensor(name, shape, dt))

        def sem(name):
            return ctx.enter_context(nc.semaphore(name))

        xs = sb("xs", [P, B, NT, D])
        xn1 = sb("xn1", [P, NT, D])
        xn1T = sb("xn1T", [P, S])
        xn2 = sb("xn2", [P, NT, D])
        xn2T = sb("xn2T", [P, S])
        qk32 = [sb("q32", [P, S]), sb("k32", [P, S])]
        hi = [sb("q_hi", [P, S], F32R), sb("k_hi", [P, S], F32R)]
        lo = [sb("q_lo", [P, S], F32R), sb("k_lo", [P, S], F32R)]
        kabs = sb("kabs", [P, S], BF16)
        q_stack = sb("q_stack", [P, 2, H // 2, HALF], F32R)
        k_stack = sb("k_stack", [P, 2, H // 2, S], F32R)
        vu = sb("vu", [P, 2, NT, 2 * D])
        v_pad = sb("v_pad", [P, 2, NT, H, 32])
        kmask = sb("kmask", [P, NT, H])
        wts = sb("wts", [P, 2, 4, BANK])
        bias_rev = wts[:].rearrange("p a j c -> p (a j c)")[:, 0:H * NEAR]
        oT = sb("oT", [P, S])
        gated = xn2
        bias_near = sb("bias_near", [P, H, NEAR])
        far_row = sb("far_row", [P, H])
        far = sb("far", [P, H])
        ext = sb("ext", [H, BANK + MAXLEN])
        mm_e = sb("mm_e", [P, E, D])
        win_s = sb("win_s", [P, 2, HC, D])
        wout_s = sb("wout_s", [P, 2, HID])
        woutT = sb("woutT", [P, 2, HC, D])
        wq_s, wk_s, wvu_s = sb("wq_s", [P, D]), sb("wk_s", [P, D]), sb("wvu_s", [P, 2 * D])
        wg_s = sb("wg_s", [P, E])
        ident = sb("ident", [P, P])
        flip = sb("flip", [P, P])
        sel = sb("sel", [P, QUADS, 4, HD])
        headsum = sb("headsum", [P, H], BF16)
        stats = sb("stats", [P, 2, NT, 6])
        mv = sb("mv", [P, 2, NT, 2])
        rstd = sb("rstd", [P, 2, NT])
        eps_t = sb("eps_t", [P, NT])
        mhalf = sb("mhalf", [P, NT])
        rank = sb("rank", [P, 1, E])
        table_in = sb("table_in", [P, 1])
        lg = sb("lg", [P, 3, NT, E])
        pick = sb("pick", [P, 2, NT, E])
        top = sb("top", [P, 5, NT])
        gate2 = sb("gate2", [P, 3, NT])
        gates = sb("gates", [P, NT, E])
        ymix = sb("ymix", [P, 2, E, D])
        rows_dram = nc.dram_tensor("rows_dram", [2, 2, H, 3 * HD, S], F32, kind="Internal").ap()
        bias_dram = nc.dram_tensor("bias_dram", [H, BANK], F32, kind="Internal").ap()

        score = [ctx.enter_context(nc.psum_tensor(f"score{j}", [P, BANK], F32)) for j in range(4)]
        o_acc = [ctx.enter_context(nc.psum_tensor(f"o_acc{j}", [P, BANK], F32)) for j in range(2)]
        jobp = [ctx.enter_context(nc.psum_tensor(f"jobp{j}", [P, BANK], F32)) for j in range(2)]

        x_in = [[sem(f"x_in{b}_{half}") for half in range(2)] for b in range(B)]
        w_qk_in, w_vu_in, w_g_in = sem("w_qk_in"), sem("w_vu_in"), sem("w_g_in")
        rb_in, far_in, ext_out, bias_in = sem("rb_in"), sem("far_in"), sem("ext_out"), sem("bias_in")
        win_in = [sem(f"win_in{i}") for i in range(2)]
        wout_in = [sem(f"wout_in{i}") for i in range(2)]
        rows_out = [[sem(f"{side}_rows_out{half}") for half in range(2)] for side in "qk"]
        stack_in = [[sem(f"stack_in{half}_{quad}") for quad in range(QUADS)] for half in range(2)]
        stored = sem("stored")
        consts = sem("consts")
        zeroed = sem("zeroed")
        ext_set, ext_ready, far_ready = sem("ext_set"), sem("ext_ready"), sem("far_ready")
        averaged = sem("averaged")
        scaled = sem("scaled")
        normed1, normed2 = sem("normed1"), sem("normed2")
        filled = sem("filled")
        drained = [sem(f"drained{i}") for i in range(8)]
        kabs_ready = sem("kabs_ready")
        hi_ready, lo_ready = sem("hi_ready"), sem("lo_ready")
        v_ready = sem("v_ready")
        scored = [sem(f"scored{j}") for j in range(4)]
        biased = [sem(f"biased{j}") for j in range(4)]
        weighed = [sem(f"weighed{j}") for j in range(4)]
        pv_done = sem("pv_done")
        o_copied = [sem(f"o_copied{i}") for i in range(2)]
        x1_ready = sem("x1_ready")
        top_ready, tanh_ready, gates_ready = sem("top_ready"), sem("tanh_ready"), sem("gates_ready")
        tile_done = sem("tile_done")
        last_done = [sem(f"last_done{k}") for k in range(HT)]
        dve_step, pool_step = sem("dve_step"), sem("pool_step")

        def wait_filled(eng, job):
            eng.wait_ge(filled, NUMBER[job] + 1)

        def wait_drained(eng, job):
            bank, earlier = bank_use(job)
            eng.wait_ge(drained[bank], earlier + 1)

        def bank_of(job):
            return (jobp + score + o_acc)[bank_use(job)[0]]

        def drained_by(ins, job):
            ins.then_inc(drained[bank_use(job)[0]], 1)

        def flipped(i):
            return bias_near[:].rearrange("p h c -> p (h c)")[:, i * BANK:(i + 1) * BANK]

        def last_mix(t):
            return wts[:].rearrange("p a j (e d) -> p (a j e) d", d=D)[:, (t - HT) * E:(t - HT + 1) * E]

        def add_last_experts(eng, then_wait, t):
            for part in range(2):
                wait_drained(eng, ("FF", B - 1, t, part))
            y = last_mix(t)
            n = E // 2
            while n >= 1:
                then_wait(eng.tensor_tensor(y[:, 0:n], y[:, 0:n], y[:, n:2 * n], ALU.add))
                n //= 2
            eng.tensor_tensor(xs[:, B - 1, t], xs[:, B - 1, t], y[:, 0], ALU.add).then_inc(last_done[t - HT], 1)

        block = ctx.enter_context(nc.Block())

        @block.sync
        def _(sp):
            def load_x(b, half):
                ts = slice(half * HT, (half + 1) * HT)
                sp.dma_start(xs[:, b, ts], x[b].rearrange("(t p) d -> p t d", p=P)[:, ts]).then_inc(x_in[b][half], 16)

            def load_expert(e):
                if e >= 2:
                    wait_filled(sp, ("M", e - 2))
                sp.dma_start(win_s[:, e % 2], w_in[e].rearrange("(c p) d -> p c d", p=P)).then_inc(win_in[e % 2], 16)
                sp.dma_start(wout_s[:, e % 2], w_out[e]).then_inc(wout_in[e % 2], 16)

            def write_rows(b, half, side):
                sp.wait_ge(hi_ready, 2 * (2 * b + half) + side + 1)
                sp.wait_ge(lo_ready, 2 * (2 * b + half) + side + 1)
                if b >= 2:
                    for quad in range(QUADS):
                        sp.wait_ge(stack_in[half][quad], 16 * STACK_DMAS * (b - 1))
                cols = slice(half * HALF, (half + 1) * HALF)
                for k, part in enumerate((hi, lo, hi)[:ROW_PARTS[side]]):
                    sp.dma_start(rows_dram[b % 2, side, :, k * HD:(k + 1) * HD, cols], part[side][:, cols].bitcast(F32))\
                        .then_inc(rows_out[side][half], 16)

            def load_stack(b, half):
                cols = slice(half * HALF, (half + 1) * HALF)
                for quad in range(QUADS):
                    if b > 0:
                        for j in range(4):
                            sp.wait_ge(scored[j], INDEX[b - 1, half, quad, len(GROUPS[half]) - 1] + 1)
                    pairs = slice(2 * quad, 2 * quad + 2)
                    for side, stack in ((0, q_stack[:, half, pairs]), (1, k_stack[:, b % 2, pairs, cols])):
                        if quad == 0:
                            sp.wait_ge(rows_out[side][half], 16 * ROW_PARTS[side] * (b + 1))
                        for odd in range(2):
                            for k in range(2):
                                first = k * HD if side else 0
                                row = 64 * odd + 32 * k
                                sp.dma_start(stack[row:row + 32].bitcast(F32),
                                             rows_dram[b % 2, side, 4 * quad + odd:4 * quad + 4:2, first:first + 32, cols]
                                             .rearrange("h r s -> r h s")).then_inc(stack_in[half][quad], 16)

            def load_unit(b, half):
                write_rows(b, half, 0)
                write_rows(b, half, 1)
                load_stack(b, half)

            def store(b, half):
                sp.wait_ge(tile_done, NT * b + HT * (half + 1))
                ts = slice(half * HT, (half + 1) * HT)
                sp.dma_start(out[b].rearrange("(t p) d -> p t d", p=P)[:, ts], xs[:, b, ts]).then_inc(stored, 16)

            load_x(0, 0)
            sp.dma_start(wq_s[:], Wq).then_inc(w_qk_in, 16)
            sp.dma_start(wk_s[:], Wk).then_inc(w_qk_in, 16)
            sp.dma_start(ext[:, BANK:BANK + MAXLEN], rel_bias[MAXLEN - 1:, :].rearrange("r h -> h r"),
                         allow_slow_non_contiguous=True).then_inc(rb_in, 16)
            sp.dma_start(far_row[:], rel_bias[2 * MAXLEN - 2:, :].to_broadcast([P, H])).then_inc(far_in, 16)
            sp.dma_start(wvu_s[:, 0:D], Wv).then_inc(w_vu_in, 16)
            sp.dma_start(wvu_s[:, D:], Wu).then_inc(w_vu_in, 16)
            sp.dma_start(wg_s[:], w_gate.rearrange("e d -> d e"), allow_slow_non_contiguous=True).then_inc(w_g_in, 16)
            load_x(0, 1)
            sp.wait_ge(ext_ready, 1)
            sp.dma_start(bias_dram, ext[:, 0:BANK]).then_inc(ext_out, 16)
            load_expert(0)
            load_expert(1)
            sp.wait_ge(ext_out, 16)
            sp.dma_start(bias_rev.rearrange("p (h c) -> p h c", h=H),
                         bass.AP(bias_dram.tensor, 0, [[1, P], [BANK, H], [1, NEAR]])).then_inc(bias_in, 16)
            load_unit(0, 0)
            for b in range(1, B):
                load_x(b, 0)
                load_x(b, 1)
            load_expert(2)
            load_expert(3)
            load_unit(0, 1)
            for e in range(4, E):
                load_expert(e)
            for b in range(1, B):
                load_unit(b, 0)
                if b > 1:
                    store(b - 2, 1)
                load_unit(b, 1)
                store(b - 1, 0)
            store(B - 2, 1)
            store(B - 1, 0)
            for t in (HT + 1, HT, HT + 2, HT + 3):
                sp.wait_ge(last_done[t - HT], 1)
                sp.dma_start(out[B - 1, t * P:(t + 1) * P], xs[:, B - 1, t]).then_inc(stored, 16)
            sp.wait_ge(stored, 16 * (2 * B - 1 + HT))

        @block.gpsimd
        def _(pool):
            step = [0]

            def then_wait(ins):
                step[0] += 1
                ins.then_inc(pool_step, 1)
                pool.wait_ge(pool_step, step[0])

            def scale(unit, ln):
                n = SCALES.index((unit, ln))
                pool.wait_ge(averaged, n + 1)
                if unit[0] > 0:
                    pool.wait_ge((normed1, normed2)[ln], 2 * (unit[0] - 1) + unit[1] + 1)
                ts = slice(unit[1] * HT, (unit[1] + 1) * HT)
                then_wait(pool.tensor_tensor(rstd[:, ln, ts], mv[:, ln, ts, 1], eps_t[:, ts], ALU.add))
                pool.tensor_tensor(rstd[:, ln, ts], rstd[:, ln, ts], mhalf[:, ts], ALU.pow).then_inc(scaled, 1)

            pool.memset(eps_t[:], EPS).then_inc(consts, 1)
            pool.memset(mhalf[:], -0.5).then_inc(consts, 1)
            then_wait(pool.memset(ident[:], 0.0))
            pool.affine_select(out=ident[:], in_=ident[:], compare_op=ALU.not_equal, fill=1.0, base=0,
                               pattern=[[-1, P]], channel_multiplier=1).then_inc(consts, 1)
            scale((0, 0), 0)
            pool.memset(v_pad[:], 0.0).then_inc(zeroed, 1)
            then_wait(pool.memset(headsum[:], 1.0))
            then_wait(pool.affine_select(out=headsum[:], in_=headsum[:], compare_op=ALU.is_ge, fill=0.0, base=0,
                                         pattern=[[-HD, H]], channel_multiplier=1))
            pool.affine_select(out=headsum[:], in_=headsum[:], compare_op=ALU.is_ge, fill=0.0, base=HD - 1,
                               pattern=[[HD, H]], channel_multiplier=-1).then_inc(consts, 1)
            then_wait(pool.memset(flip[:], 0.0))
            pool.affine_select(out=flip[:], in_=flip[:], compare_op=ALU.not_equal, fill=1.0, base=1 - P,
                               pattern=[[1, P]], channel_multiplier=1).then_inc(consts, 1)
            then_wait(pool.memset(sel[:], 0.0))
            pool.affine_select(out=sel[:], in_=sel[:], compare_op=ALU.not_equal, fill=1.0, base=0,
                               pattern=[[-HD, QUADS], [-32, 4], [-1, HD]], channel_multiplier=1).then_inc(consts, 1)
            for e in range(E):
                pool.memset(rank[:, :, e:e + 1], float(E - e)).then_inc(consts, 1)

            def split_lo(b, half):
                cols = slice(half * HALF, (half + 1) * HALF)
                for side in range(2):
                    pool.wait_ge(hi_ready, 2 * (2 * b + half) + side + 1)
                    pool.tensor_tensor(lo[side][:, cols], qk32[side][:, cols], hi[side][:, cols].bitcast(F32),
                                       ALU.subtract).then_inc(lo_ready, 1)

            def mask_v(b, half):
                wait_drained(pool, ("MASK", b, half))
                wait_drained(pool, ("VU", b, 2 * half))
                wait_drained(pool, ("VU", b, 2 * half + 1))
                if b == 0 and half == 0:
                    pool.wait_ge(zeroed, 1)
                if b >= 2:
                    pool.wait_ge(pv_done, unit_end(b - 2, 1))
                ts = slice(half * HT, (half + 1) * HT)
                for quad in range(QUADS):
                    hs = slice(4 * quad, 4 * quad + 4)
                    pool.tensor_tensor(v_pad[:, b % 2, ts, hs, HD * quad:HD * quad + HD],
                                       vu[:, b % 2, ts, 4 * quad * HD:4 * (quad + 1) * HD].rearrange("p t (h d) -> p t h d", h=4),
                                       kmask[:, ts, hs].unsqueeze(3).to_broadcast([P, HT, 4, HD]), ALU.mult)\
                        .then_inc(v_ready, 1)

            def add_attention(b, half):
                wait_drained(pool, ("SEL", b, half))
                ts = slice(half * HT, (half + 1) * HT)
                pool.tensor_tensor(xs[:, b, ts], xs[:, b, ts], gated[:, ts], ALU.add).then_inc(x1_ready, 1)

            def add_experts(b, t):
                wait_drained(pool, ("FF", b, t, 0))
                wait_drained(pool, ("FF", b, t, 1))
                y = ymix[:, t % 2]
                n = E // 2
                while n >= 1:
                    then_wait(pool.tensor_tensor(y[:, 0:n], y[:, 0:n], y[:, n:2 * n], ALU.add))
                    n //= 2
                pool.tensor_tensor(xs[:, b, t], xs[:, b, t], y[:, 0], ALU.add).then_inc(tile_done, 1)

            def jobs(i):
                for job in TIMELINE[i][1]:
                    kind = job[0]
                    if kind in ("stats1", "stats2") and i > 0:
                        scale(job[1:], int(kind == "stats2"))
                    elif kind == "split" and i >= PROLOGUE:
                        split_lo(job[1], job[2])
                    elif kind == "MASK":
                        mask_v(job[1], job[2])
                    elif kind == "SEL" and job[1:] != (B - 1, 1):
                        add_attention(job[1], job[2])
                    elif kind == "FF" and job[3] == 1:
                        if i < len(TIMELINE) - 1:
                            add_experts(job[1], job[2])
                        elif job[2] in POOL_SUMS:
                            add_last_experts(pool, then_wait, job[2])

            for i in range(len(TIMELINE)):
                jobs(i)

        @block.tensor
        def _(pe):
            def scores(group, j):
                b, half, quad, g = group
                kb, q0, n = GROUPS[half][g]
                h = 4 * quad + j
                rows = slice(64 * (h % 2), 64 * (h % 2) + 64)
                if g == 0 and j == 0:
                    pe.wait_ge(stack_in[half][quad], 16 * STACK_DMAS * (b + 1))
                if INDEX[group] > 0:
                    pe.wait_ge(weighed[j], INDEX[group])
                pe.matmul(score[j][:, 0:n], k_stack[rows, b % 2, h // 2, kb * P:(kb + 1) * P],
                          q_stack[rows, half, h // 2, q0 - half * HALF:q0 - half * HALF + n],
                          start=True, stop=True).then_inc(scored[j], 1)

            def times_v(group):
                b, half, quad, g = group
                kb, q0, n = GROUPS[half][g]
                c0 = q0 - half * HALF
                if quad == 0 and g == 0:
                    pe.wait_ge(v_ready, QUADS * (2 * b + half + 1))
                    if b > 0:
                        pe.wait_ge(o_copied[half], b)
                for j in range(4):
                    pe.wait_ge(weighed[j], INDEX[group] + 1)
                for j in range(4):
                    ins = pe.matmul(o_acc[half][32 * j:32 * j + 32, c0:c0 + n], v_pad[:, b % 2, kb, 4 * quad + j, :],
                                    wts[:, INDEX[group] % 2, j, 0:n], start=(quad == 0 and g == 0),
                                    stop=(INDEX[group] + 1 == unit_end(b, half)))
                ins.then_inc(pv_done, 1)

            def job_pe(job):
                kind, args = job[0], job[1:]
                if kind not in BANKED:
                    return
                bank, (index, earlier) = bank_of(job), bank_use(job)
                if earlier:
                    pe.wait_ge(drained[index], earlier)
                elif 2 <= index < 6:
                    pe.wait_ge(weighed[index - 2], len(ORDER))
                elif index >= 6:
                    pe.wait_ge(o_copied[index - 6], B)
                if kind in ("T1", "T2"):
                    b, half = args
                    src, ready = (xn1, normed1) if kind == "T1" else (xn2, normed2)
                    if NUMBER[job] == 0:
                        pe.wait_ge(consts, 3)
                    pe.wait_ge(ready, 2 * b + half + 1)
                    for k in range(HT):
                        ins = pe.transpose(bank[:, k * P:(k + 1) * P], src[:, HT * half + k, :], ident[:])
                elif kind in ("Q", "K"):
                    b, half = args
                    pe.wait_ge(w_qk_in, 32)
                    wait_drained(pe, ("T1", b, half))
                    ins = pe.matmul(bank[:], (wq_s if kind == "Q" else wk_s)[:], xn1T[:, half * HALF:(half + 1) * HALF],
                                    start=True, stop=True)
                elif kind == "VU":
                    b, i = args
                    pe.wait_ge(w_vu_in, 32)
                    for k in range(2):
                        t = 2 * i + k
                        ins = pe.matmul(bank[:, k * 2 * D:(k + 1) * 2 * D], xn1T[:, t * P:(t + 1) * P], wvu_s[:],
                                        start=True, stop=True)
                elif kind == "MASK":
                    b, half = args
                    if b == 0 and half == 0:
                        pe.wait_ge(consts, 4)
                    pe.wait_ge(kabs_ready, 2 * b + half + 1)
                    for k in range(HT):
                        t = HT * half + k
                        ins = pe.matmul(bank[:, k * H:(k + 1) * H], kabs[:, t * P:(t + 1) * P], headsum[:],
                                        start=True, stop=True)
                elif kind == "SEL":
                    b, half = args
                    if b == 0 and half == 0:
                        pe.wait_ge(consts, 6)
                    pe.wait_ge(o_copied[half], b + 1)
                    for k in range(HT):
                        t = HT * half + k
                        ins = pe.matmul(bank[:, k * D:(k + 1) * D], oT[:, t * P:(t + 1) * P],
                                        sel[:].rearrange("p q j d -> p (q j d)"), start=True, stop=True)
                elif kind == "LOG":
                    b, half = args
                    pe.wait_ge(w_g_in, 16)
                    wait_drained(pe, ("T2", b, half))
                    for k in range(HT):
                        t = HT * half + k
                        ins = pe.matmul(bank[:, k * E:(k + 1) * E], xn2T[:, t * P:(t + 1) * P], wg_s[:],
                                        start=True, stop=True)
                elif kind == "FF":
                    b, t, part = args
                    if b == 0 and t == 0:
                        wait_drained(pe, ("M", E - 1))
                        wait_drained(pe, ("M", E - 2))
                    ins = pe.matmul(bank[:], xn2T[:, t * P:(t + 1) * P],
                                    mm_e[:, part * E // 2:(part + 1) * E // 2, :].rearrange("p e d -> p (e d)"),
                                    start=True, stop=True)
                elif kind == "FLIP":
                    i = args[0]
                    pe.wait_ge(bias_in, 16)
                    pe.wait_ge(consts, 5)
                    ins = pe.matmul(bank[:], flip[:], bias_rev[:, i * BANK:(i + 1) * BANK], start=True, stop=True)
                elif kind == "WT":
                    e = args[0]
                    pe.wait_ge(wout_in[e % 2], 16 * (e // 2 + 1))
                    for c in range(HC):
                        ins = pe.transpose(bank[:, c * P:(c + 1) * P], wout_s[:, e % 2, c * P:(c + 1) * P], ident[:])
                elif kind == "M":
                    e = args[0]
                    pe.wait_ge(win_in[e % 2], 16 * (e // 2 + 1))
                    wait_drained(pe, ("WT", e))
                    for c in range(HC):
                        ins = pe.matmul(bank[:, 0:D], win_s[:, e % 2, c, :], woutT[:, e % 2, c, :],
                                        start=(c == 0), stop=(c == HC - 1))
                ins.then_inc(filled, 1)

            for i, (group, jobs) in enumerate(TIMELINE):
                before = TIMELINE[i - 1][0] if i > 0 else None
                after = TIMELINE[i + 1][0] if i + 1 < len(TIMELINE) else None
                if group and after:
                    scores(after, 0)
                if before:
                    times_v(before)
                if group and after:
                    scores(after, 1)
                for job in first_job(jobs):
                    job_pe(job)
                if group and after:
                    scores(after, 2)
                for job in later_jobs(jobs):
                    job_pe(job)
                if group and after:
                    scores(after, 3)
                if after and not group:
                    for j in range(4):
                        scores(after, j)

        @block.scalar
        def _(act):
            def weigh(group, j):
                b, half, quad, g = group
                kb, q0, n = GROUPS[half][g]
                number = INDEX[group]
                if number == 0 and j == 0:
                    act.wait_ge(far_ready, 1)
                if group in BIASED:
                    act.wait_ge(biased[j], BIASED[group] + 1)
                else:
                    act.wait_ge(scored[j], number + 1)
                if number >= 2 and j == 0:
                    act.wait_ge(pv_done, number - 1)
                h = 4 * quad + j
                act.activation(wts[:, number % 2, j, 0:n], score[j][:, 0:n], ACT.Silu,
                               bias=far[:, h:h + 1], scale=HD ** -0.5).then_inc(weighed[j], 1)

            def job_act(job):
                kind, args = job[0], job[1:]
                if kind == "FF" and args[0] == B - 1 and args[1] in ACT_SCALES:
                    b, t, part = args
                    wait_filled(act, job)
                    act.wait_ge(gates_ready, 2 * B)
                    act.wait_ge(pv_done, len(ORDER))
                    for e in range(part * E // 2, (part + 1) * E // 2):
                        ins = act.activation(last_mix(t)[:, e], bank_of(job)[:].rearrange("p (e d) -> p e d", d=D)[:, e % (E // 2)],
                                             ACT.Copy, scale=gates[:, t, e:e + 1])
                    drained_by(ins, job)
                elif kind in ("T1", "T2"):
                    b, half = args
                    wait_filled(act, job)
                    if b > 0:
                        wait_filled(act, ("VU", b - 1, 2 * half + 1) if kind == "T1" else ("FF", b - 1, HT * (half + 1) - 1, 1))
                    dst = xn1T if kind == "T1" else xn2T
                    drained_by(act.copy(dst[:, half * HALF:(half + 1) * HALF], bank_of(job)[:]), job)
                elif kind in ("Q", "K"):
                    b, half = args
                    side = int(kind == "K")
                    wait_filled(act, job)
                    if b > 0:
                        act.wait_ge(lo_ready, 2 * (2 * (b - 1) + half) + side + 1)
                        if side:
                            wait_filled(act, ("MASK", b - 1, half))
                    cols = slice(half * HALF, (half + 1) * HALF)
                    drained_by(act.activation(qk32[side][:, cols], bank_of(job)[:], ACT.Silu), job)
                    if side:
                        wait_drained(act, job)
                        act.activation(kabs[:, cols], qk32[1][:, cols], ACT.Abs).then_inc(kabs_ready, 1)
                elif kind == "VU":
                    b, i = args
                    wait_filled(act, job)
                    if b >= 2:
                        act.wait_ge(v_ready, QUADS * (2 * (b - 2) + i // 2 + 1))
                        wait_drained(act, ("SEL", b - 2, i // 2))
                    drained_by(act.activation(vu[:, b % 2, 2 * i:2 * i + 2, :].rearrange("p t d -> p (t d)"),
                                              bank_of(job)[:], ACT.Silu), job)
                elif kind == "gates":
                    b, half = args
                    ts = slice(half * HT, (half + 1) * HT)
                    act.wait_ge(top_ready, 2 * b + half + 1)
                    act.activation(gate2[:, 0, ts], top[:, 4, ts], ACT.Tanh, scale=0.5).then_inc(tanh_ready, 1)
                elif kind == "FLIP" and args[0] % 2 == 1:
                    wait_filled(act, job)
                    drained_by(act.copy(flipped(args[0]), bank_of(job)[:]), job)
                elif kind == "WT":
                    e = args[0]
                    wait_filled(act, job)
                    if e >= 2:
                        wait_filled(act, ("M", e - 2))
                    drained_by(act.copy(woutT[:, e % 2].rearrange("p c d -> p (c d)"), bank_of(job)[:]), job)
                elif kind == "M":
                    wait_filled(act, job)
                    drained_by(act.copy(mm_e[:, args[0], :], bank_of(job)[:, 0:D]), job)

            act.wait_ge(consts, 1)
            act.activation(table_in[:], eps_t[:, 0:1], ACT.Silu)
            for i, (group, jobs) in enumerate(TIMELINE):
                if group:
                    weigh(group, 0)
                if i > 0 and TIMELINE[i - 1][0]:
                    for job in first_job(TIMELINE[i - 1][1]):
                        job_act(job)
                if group:
                    weigh(group, 1)
                if i > 0 and TIMELINE[i - 1][0]:
                    for job in later_jobs(TIMELINE[i - 1][1]):
                        job_act(job)
                if group:
                    weigh(group, 2)
                    weigh(group, 3)
                else:
                    for job in jobs:
                        job_act(job)

        @block.vector
        def _(dve):
            step = [0]

            def then_wait(ins):
                step[0] += 1
                ins.then_inc(dve_step, 1)
                dve.wait_ge(dve_step, step[0])

            def add_bias(group, j):
                b, half, quad, g = group
                kb, q0, n = GROUPS[half][g]
                if group not in BIASED:
                    return
                c0 = q0 - kb * P
                near = min(n, NEAR - c0)
                if INDEX[group] == 0:
                    for i in range(2):
                        wait_drained(dve, ("FLIP", FLIPS - 1 - i))
                dve.wait_ge(scored[j], INDEX[group] + 1)
                dve.tensor_tensor(score[j][:, 0:near], score[j][:, 0:near], bias_near[:, 4 * quad + j, c0:c0 + near],
                                  ALU.add).then_inc(biased[j], 1)

            def copy_outputs(group):
                b, half, quad, g = group
                if INDEX[group] + 1 != unit_end(b, half):
                    return
                dve.wait_ge(pv_done, INDEX[group] + 1)
                if b > 0:
                    wait_filled(dve, ("SEL", b - 1, half))
                dve.tensor_copy(oT[:, half * HALF:(half + 1) * HALF], o_acc[half][:]).then_inc(o_copied[half], 1)

            def job_dve(job):
                kind, args = job[0], job[1:]
                if kind in ("stats1", "stats2"):
                    b, half = args
                    ln = int(kind == "stats2")
                    if ln:
                        dve.wait_ge(x1_ready, 2 * b + half + 1)
                    else:
                        dve.wait_ge(x_in[b][half], 16)
                    for t in range(HT * half, HT * (half + 1)):
                        ins = dve.bn_stats(stats[:, ln, t, :], xs[:, b, t, :])
                    then_wait(ins)
                    for t in range(HT * half, HT * (half + 1)):
                        ins = dve.bn_aggr(mv[:, ln, t, :], stats[:, ln, t, :])
                    ins.then_inc(averaged, 1)
                elif kind in ("norm1", "norm2"):
                    b, half = args
                    ln = int(kind == "norm2")
                    dve.wait_ge(scaled, SCALES.index((args, ln)) + 1)
                    if b > 0:
                        wait_filled(dve, (("T1", "T2")[ln], b - 1, half))
                    dst = xn2 if ln else xn1
                    for t in range(HT * half, HT * (half + 1)):
                        ins = dve.tensor_scalar(dst[:, t, :], xs[:, b, t, :], mv[:, ln, t, 0:1], rstd[:, ln, t:t + 1],
                                                ALU.subtract, ALU.mult)
                    ins.then_inc((normed1, normed2)[ln], 1)
                elif kind == "split":
                    b, half = args
                    cols = slice(half * HALF, (half + 1) * HALF)
                    for side in range(2):
                        if b > 0:
                            dve.wait_ge(rows_out[side][half], 16 * ROW_PARTS[side] * b)
                        wait_drained(dve, ("QK"[side], b, half))
                        ins = dve.tensor_copy(hi[side][:, cols], qk32[side][:, cols])
                        ins.then_inc(hi_ready, 1)
                        if b == 0 and half == 0:
                            dve.wait_ge(hi_ready, side + 1)
                            dve.tensor_tensor(lo[side][:, cols], qk32[side][:, cols], hi[side][:, cols].bitcast(F32),
                                              ALU.subtract).then_inc(lo_ready, 1)
                elif kind == "MASK":
                    b, half = args
                    wait_filled(dve, job)
                    if b > 0:
                        dve.wait_ge(v_ready, QUADS * (2 * (b - 1) + half + 1))
                    ts = slice(half * HT, (half + 1) * HT)
                    drained_by(dve.tensor_scalar(kmask[:, ts].rearrange("p t h -> p (t h)"), bank_of(job)[:, 0:HT * H],
                                                 0.0, None, ALU.not_equal), job)
                elif kind == "FLIP" and args[0] % 2 == 0:
                    wait_filled(dve, job)
                    drained_by(dve.tensor_copy(flipped(args[0]), bank_of(job)[:]), job)
                elif kind == "SEL":
                    b, half = args
                    wait_filled(dve, job)
                    if b > 0:
                        wait_filled(dve, ("T2", b - 1, half))
                    ts = slice(half * HT, (half + 1) * HT)
                    drained_by(dve.tensor_tensor(gated[:, ts], bank_of(job)[:].rearrange("p (t d) -> p t d", d=D),
                                                 vu[:, b % 2, ts, D:], ALU.mult), job)
                    if (b, half) == (B - 1, 1):
                        wait_drained(dve, job)
                        dve.tensor_tensor(xs[:, b, ts], xs[:, b, ts], gated[:, ts], ALU.add).then_inc(x1_ready, 1)
                elif kind == "LOG":
                    b, half = args
                    wait_filled(dve, job)
                    ts = slice(half * HT, (half + 1) * HT)
                    drained_by(dve.tensor_copy(lg[:, 0, ts].rearrange("p t e -> p (t e)"), bank_of(job)[:, 0:HT * E]), job)
                elif kind == "best":
                    take_best(*args)
                elif kind == "gates":
                    mix_gates(*args)
                elif kind == "FF":
                    b, t, part = args
                    last = (b, t // HT) == (B - 1, 1)
                    if last and part == 1 and t not in POOL_SUMS:
                        if t not in ACT_SCALES:
                            scale_experts(job, last_mix(t))
                        add_last_experts(dve, then_wait, t)
                    elif last and t not in ACT_SCALES:
                        if NUMBER[job] == NUMBER["FF", b, LAST_TILES[0], 0]:
                            dve.wait_ge(pv_done, len(ORDER))
                        scale_experts(job, last_mix(t))
                    elif not last:
                        if NT * b + t >= 2:
                            dve.wait_ge(tile_done, NT * b + t - 1)
                        scale_experts(job, ymix[:, t % 2])

            def scale_experts(job, y):
                kind, b, t, part = job
                wait_filled(dve, job)
                es = slice(part * E // 2, (part + 1) * E // 2)
                drained_by(dve.tensor_tensor(y[:, es], bank_of(job)[:].rearrange("p (e d) -> p e d", d=D),
                                             gates[:, t, es].unsqueeze(2).to_broadcast([P, E // 2, D]), ALU.mult), job)

            def wide(a):
                return a.unsqueeze(2).to_broadcast([P, HT, E])

            def take_best(b, half, r):
                ts = slice(half * HT, (half + 1) * HT)
                if r == 0:
                    wait_drained(dve, ("LOG", b, half))
                if r == 0 and b == 0 and half == 0:
                    dve.wait_ge(consts, 6 + E)
                if r == 1:
                    then_wait(dve.scalar_tensor_tensor(lg[:, 1, ts], pick[:, 0, ts], -1e38, lg[:, 0, ts], ALU.mult, ALU.add))
                then_wait(dve.tensor_reduce(top[:, r, ts], lg[:, r, ts], AX, ALU.max))
                then_wait(dve.tensor_tensor(lg[:, 2, ts], lg[:, r, ts], wide(top[:, r, ts]), ALU.is_equal))
                then_wait(dve.tensor_tensor(lg[:, 2, ts], lg[:, 2, ts], rank[:].to_broadcast([P, HT, E]), ALU.mult))
                then_wait(dve.tensor_reduce(top[:, 2 + r, ts], lg[:, 2, ts], AX, ALU.max))
                then_wait(dve.tensor_tensor(pick[:, r, ts], lg[:, 2, ts], wide(top[:, 2 + r, ts]), ALU.is_equal))
                if r == 1:
                    dve.tensor_tensor(top[:, 4, ts], top[:, 0, ts], top[:, 1, ts], ALU.subtract).then_inc(top_ready, 1)

            def mix_gates(b, half):
                ts = slice(half * HT, (half + 1) * HT)
                dve.wait_ge(tanh_ready, 2 * b + half + 1)
                dve.tensor_scalar(gate2[:, 2, ts], gate2[:, 0, ts], -0.5, 0.5, ALU.mult, ALU.add)
                then_wait(dve.tensor_scalar(gate2[:, 1, ts], gate2[:, 0, ts], 0.5, 0.5, ALU.mult, ALU.add))
                dve.tensor_tensor(pick[:, 0, ts], pick[:, 0, ts], wide(gate2[:, 1, ts]), ALU.mult)
                then_wait(dve.tensor_tensor(pick[:, 1, ts], pick[:, 1, ts], wide(gate2[:, 2, ts]), ALU.mult))
                dve.tensor_tensor(gates[:, ts], pick[:, 0, ts], pick[:, 1, ts], ALU.add).then_inc(gates_ready, 1)
                dve.wait_ge(gates_ready, 2 * b + half + 1)

            def set_biases():
                then_wait(dve.memset(ext[:, 0:P - 1], NEG))
                then_wait(dve.memset(ext[:, P - 1 + MAXLEN:BANK], 0.0))
                dve.wait_ge(rb_in, 16)
                dve.tensor_scalar(ext[:, P - 1:P - 1 + MAXLEN], ext[:, BANK:BANK + MAXLEN],
                                  ext[:, BANK + MAXLEN - 1:BANK + MAXLEN], None, ALU.subtract).then_inc(ext_ready, 1)
                dve.wait_ge(far_in, 16)
                dve.tensor_scalar(far[:], far_row[:], HD ** -0.5, None, ALU.mult).then_inc(far_ready, 1)

            for i, (group, jobs) in enumerate(TIMELINE):
                before = TIMELINE[i - 1][0] if i > 0 else None
                after = TIMELINE[i + 1][0] if i + 1 < len(TIMELINE) else None
                if not group:
                    if before:
                        for job in later_jobs(TIMELINE[i - 1][1]):
                            job_dve(job)
                        copy_outputs(before)
                    for job in jobs:
                        job_dve(job)
                    if i == 0:
                        set_biases()
                if after:
                    add_bias(after, 0)
                if group and before:
                    for job in later_jobs(TIMELINE[i - 1][1]):
                        job_dve(job)
                if after:
                    add_bias(after, 1)
                if group:
                    for job in first_job(jobs):
                        job_dve(job)
                if after:
                    add_bias(after, 2)
                    add_bias(after, 3)
                if group and before:
                    copy_outputs(before)


SCALES = [(j[1:], int(j[0] == "stats2")) for _, jobs in TIMELINE for j in jobs if j[0] in ("stats1", "stats2")]
BIASED = {}
for _group in ORDER:
    _kb, _q0, _n = GROUPS[_group[1]][_group[3]]
    if _kb * P + NEAR > _q0:
        BIASED[_group] = len(BIASED)

_INS = ["L0_attn_x", "L0_attn_Wq", "L0_attn_Wk", "L0_attn_Wv", "L0_attn_Wu", "L0_attn_rel_bias",
        "L0_ffn_w_gate", "L0_ffn_w_in", "L0_ffn_w_out"]


def kernel(**inputs):
    import numpy as _np
    import concourse.bacc as _bacc
    from concourse import mybir as _mybir
    from concourse.bass_utils import run_bass_kernel_spmd as _run

    nc = _bacc.Bacc("TRN2", target_bir_lowering=False, num_devices=1)
    arrays, args = {}, []
    for name in _INS:
        a = _np.ascontiguousarray(inputs[name])
        arrays[f"in_{name}"] = a
        args.append(nc.dram_tensor(f"in_{name}", a.shape, _mybir.dt.from_np(a.dtype), kind="ExternalInput").ap())
    out = nc.dram_tensor("out_0", [B, S, D], _mybir.dt.float32, kind="ExternalOutput").ap()
    build(nc, *args, out)
    r = _run(nc, [arrays], core_ids=[0])
    return r.results[0]["out_0"]
```
